# Optimizing a Trainium2 kernel written in Bass

```python
import numpy as np
import jax
import jax.numpy as jnp

def _softmax(x, axis=-1):
    return jax.nn.softmax(x, axis=axis)

def _gelu(x):
    return jax.nn.gelu(x, approximate=True)

def _silu(x):
    return jax.nn.silu(x)

def _sigmoid(x):
    return jax.nn.sigmoid(x)

def _layernorm(x, axis=-1, eps=1e-05):
    m = jnp.mean(x, axis=axis, keepdims=True)
    v = jnp.var(x, axis=axis, keepdims=True)
    return (x - m) / jnp.sqrt(v + eps)

def _scatter_add(tgt, idx, src, axis=0):
    return tgt.at[idx].add(src)

def _segment_sum(src, seg, n):
    return jax.ops.segment_sum(src, seg, n)
kernel_name = 'mk_seq_postln_d1_jaxref_r4_085bc8'

def setup_inputs(seed: int=0):
    np.random.seed(seed)
    _w = jnp.asarray

    def _L0_attn_setup():
        import jax, jax.numpy as jnp
        import numpy as np
        D_MODEL = 256
        NUM_HEADS = 16
        D_HEAD = D_MODEL // NUM_HEADS
        LN_EPS = 1e-05

        def apply_rope(x):
            L = x.shape[2]
            inv_freq = 1.0 / 10000.0 ** (jnp.arange(0, D_HEAD, 2, dtype=jnp.float32) / D_HEAD)
            freqs = jnp.arange(L, dtype=jnp.float32)[:, None] * inv_freq[None, :]
            sin = jnp.sin(freqs)[None, None]
            cos = jnp.cos(freqs)[None, None]
            x1 = x[..., ::2]
            x2 = x[..., 1::2]
            rot = jnp.stack([x1 * cos - x2 * sin, x1 * sin + x2 * cos], axis=-1)
            return rot.reshape(x.shape)
        key = jax.random.key(seed)
        ks = jax.random.split(key, 10)
        B, L = (4, 512)
        s = 1.0 / np.sqrt(D_MODEL)
        inp = {'x': jax.random.normal(ks[0], (B, L, D_MODEL), dtype=jnp.float32), 'ln_gamma': jnp.ones((D_MODEL,), jnp.float32), 'ln_beta': jnp.zeros((D_MODEL,), jnp.float32), 'Wq': jax.random.normal(ks[1], (D_MODEL, D_MODEL), jnp.float32) * s, 'bq': jnp.zeros((D_MODEL,), jnp.float32), 'Wk': jax.random.normal(ks[2], (D_MODEL, D_MODEL), jnp.float32) * s, 'bk': jnp.zeros((D_MODEL,), jnp.float32), 'Wv': jax.random.normal(ks[3], (D_MODEL, D_MODEL), jnp.float32) * s, 'bv': jnp.zeros((D_MODEL,), jnp.float32), 'Wo': jax.random.normal(ks[4], (D_MODEL, D_MODEL), jnp.float32) * s, 'bo': jnp.zeros((D_MODEL,), jnp.float32)}
        return inp
    _L0_attn_in = _L0_attn_setup()

    def _L0_ffn_setup():
        import jax, jax.numpy as jnp
        import numpy as np
        DIM = 256

        def _reference_tuple_inner(x, W_r, W_k, W_v, mu_r, mu_k):
            B, T, C = x.shape
            x_prev = jnp.concatenate([jnp.zeros((B, 1, C), x.dtype), x[:, :-1, :]], axis=1)
            xr = mu_r * x + (1.0 - mu_r) * x_prev
            xk = mu_k * x + (1.0 - mu_k) * x_prev
            r = jax.nn.sigmoid(jnp.einsum('btc,dc->btd', xr, W_r))
            k = jnp.einsum('btc,dc->btd', xk, W_k)
            k_act = jnp.square(jax.nn.relu(k))
            out = r * jnp.einsum('btc,dc->btd', k_act, W_v)
            new_state = x[:, -1, :]
            return (out, new_state)
        key = jax.random.key(seed)
        ks = jax.random.split(key, 6)
        B, T, C = (8, 512, DIM)
        x = jax.random.normal(ks[0], (B, T, C), dtype=jnp.float32)
        s = 1.0 / np.sqrt(C)
        W_r = jax.random.uniform(ks[1], (C, C), jnp.float32, -s, s)
        W_k = jax.random.uniform(ks[2], (C, C), jnp.float32, -s, s)
        W_v = jax.random.uniform(ks[3], (C, C), jnp.float32, -s, s)
        mu_r = jax.random.uniform(ks[4], (C,), jnp.float32)
        mu_k = jax.random.uniform(ks[5], (C,), jnp.float32)
        return {'x': x, 'W_r': W_r, 'W_k': W_k, 'W_v': W_v, 'mu_r': mu_r, 'mu_k': mu_k}
    _L0_ffn_in = _L0_ffn_setup()
    _d = {'L0_attn_x': _L0_attn_in['x'], 'L0_attn_ln_gamma': _L0_attn_in['ln_gamma'], 'L0_attn_ln_beta': _L0_attn_in['ln_beta'], 'L0_attn_Wq': _L0_attn_in['Wq'], 'L0_attn_bq': _L0_attn_in['bq'], 'L0_attn_Wk': _L0_attn_in['Wk'], 'L0_attn_bk': _L0_attn_in['bk'], 'L0_attn_Wv': _L0_attn_in['Wv'], 'L0_attn_bv': _L0_attn_in['bv'], 'L0_attn_Wo': _L0_attn_in['Wo'], 'L0_attn_bo': _L0_attn_in['bo'], 'L0_ffn_W_r': _L0_ffn_in['W_r'], 'L0_ffn_W_k': _L0_ffn_in['W_k'], 'L0_ffn_W_v': _L0_ffn_in['W_v'], 'L0_ffn_mu_r': _L0_ffn_in['mu_r'], 'L0_ffn_mu_k': _L0_ffn_in['mu_k']}
    _x0 = _d['L0_attn_x']
    _d['L0_attn_x'] = jax.random.normal(jax.random.fold_in(jax.random.key(seed), 1), (8, 1024, 256), dtype=_x0.dtype)
    del _x0
    return _d

def reference(L0_attn_x, L0_attn_ln_gamma, L0_attn_ln_beta, L0_attn_Wq, L0_attn_bq, L0_attn_Wk, L0_attn_bk, L0_attn_Wv, L0_attn_bv, L0_attn_Wo, L0_attn_bo, L0_ffn_W_r, L0_ffn_W_k, L0_ffn_W_v, L0_ffn_mu_r, L0_ffn_mu_k):

    def _L0_attn_ref(x, ln_gamma, ln_beta, Wq, bq, Wk, bk, Wv, bv, Wo, bo):
        import jax, jax.numpy as jnp
        import numpy as np
        D_MODEL = 256
        NUM_HEADS = 16
        D_HEAD = D_MODEL // NUM_HEADS
        LN_EPS = 1e-05

        def apply_rope(x):
            L = x.shape[2]
            inv_freq = 1.0 / 10000.0 ** (jnp.arange(0, D_HEAD, 2, dtype=jnp.float32) / D_HEAD)
            freqs = jnp.arange(L, dtype=jnp.float32)[:, None] * inv_freq[None, :]
            sin = jnp.sin(freqs)[None, None]
            cos = jnp.cos(freqs)[None, None]
            x1 = x[..., ::2]
            x2 = x[..., 1::2]
            rot = jnp.stack([x1 * cos - x2 * sin, x1 * sin + x2 * cos], axis=-1)
            return rot.reshape(x.shape)
        B, L, _ = x.shape
        mu = jnp.mean(x, axis=-1, keepdims=True)
        var = jnp.mean(jnp.square(x - mu), axis=-1, keepdims=True)
        xn = (x - mu) * jax.lax.rsqrt(var + LN_EPS) * ln_gamma + ln_beta

        def heads(t):
            return t.reshape(B, L, NUM_HEADS, D_HEAD).transpose(0, 2, 1, 3)
        q = heads(xn @ Wq + bq)
        k = heads(xn @ Wk + bk)
        v = heads(xn @ Wv + bv)
        q = apply_rope(q)
        k = apply_rope(k)
        scores = jnp.einsum('bhid,bhjd->bhij', q, k) / jnp.sqrt(jnp.float32(D_HEAD))
        mask = jnp.tril(jnp.ones((L, L), jnp.float32))[None, None]
        scores = scores * mask + (1.0 - mask) * -1000000000.0
        probs = jax.nn.softmax(scores, axis=-1)
        out = jnp.einsum('bhij,bhjd->bhid', probs, v)
        out = out.transpose(0, 2, 1, 3).reshape(B, L, D_MODEL)
        out = out @ Wo + bo
        return x + out

    def _L0_ffn_ref(x, W_r, W_k, W_v, mu_r, mu_k):
        import jax, jax.numpy as jnp
        import numpy as np
        DIM = 256

        def _reference_tuple_inner(x, W_r, W_k, W_v, mu_r, mu_k):
            B, T, C = x.shape
            x_prev = jnp.concatenate([jnp.zeros((B, 1, C), x.dtype), x[:, :-1, :]], axis=1)
            xr = mu_r * x + (1.0 - mu_r) * x_prev
            xk = mu_k * x + (1.0 - mu_k) * x_prev
            r = jax.nn.sigmoid(jnp.einsum('btc,dc->btd', xr, W_r))
            k = jnp.einsum('btc,dc->btd', xk, W_k)
            k_act = jnp.square(jax.nn.relu(k))
            out = r * jnp.einsum('btc,dc->btd', k_act, W_v)
            new_state = x[:, -1, :]
            return (out, new_state)
        return _reference_tuple_inner(x, W_r, W_k, W_v, mu_r, mu_k)[0]
    x = L0_attn_x
    x = _layernorm(x + _L0_attn_ref(x, L0_attn_ln_gamma, L0_attn_ln_beta, L0_attn_Wq, L0_attn_bq, L0_attn_Wk, L0_attn_bk, L0_attn_Wv, L0_attn_bv, L0_attn_Wo, L0_attn_bo), axis=-1)
    x = _layernorm(x + _L0_ffn_ref(x, L0_ffn_W_r, L0_ffn_W_k, L0_ffn_W_v, L0_ffn_mu_r, L0_ffn_mu_k), axis=-1)
    return x

_drawn_inputs = setup_inputs


def setup_inputs(seed=0):
    import zlib

    import numpy as np

    out = dict(_drawn_inputs(seed))
    spreads = {'L0_attn_ln_gamma': (1.0, 0.6),
     'L0_attn_ln_beta': (0.0, 0.1),
     'L0_attn_bq': (0.0, 0.8),
     'L0_attn_bk': (0.0, 0.8),
     'L0_attn_bv': (0.0, 0.1),
     'L0_attn_bo': (0.0, 0.1)}
    factors = {'L0_ffn_W_r': 3.149, 'L0_ffn_mu_r': 6.377}
    for name, (base, spread) in spreads.items():
        noise = np.random.default_rng([zlib.crc32(name.encode()), seed]).standard_normal(out[name].shape)
        drawn = base * np.exp(spread * noise) if base else spread * noise
        out[name] = jnp.asarray(drawn.astype(out[name].dtype))
    for name, factor in factors.items():
        out[name] = (out[name] * factor).astype(out[name].dtype)
    return out
```

```python
from contextlib import ExitStack

import concourse.bass as bass
from concourse import mybir

F32 = mybir.dt.float32
BF16 = mybir.dt.bfloat16
ALU = mybir.AluOpType
ACT = mybir.ActivationFunctionType
AX = mybir.AxisListType

P = 128
B, L, D = 8, 1024, 256
H, DH = 16, 16
HG = 4
NG = H // HG
NT = L // P
CH = 512
CT = CH // P
HALVES = L // CH
KC = D // P
PAIR = DH // 2
EPS = 1e-5
LOWEST = -3.0e38
START = 1
STACK = 6 * DH
SHIFT = 3
VW = 32

Q_RUNS = [(0, 0, 3), (3 * DH, 0, 2), (5 * DH, 0, 1)]
K_RUNS = [(0, 0, 1), (DH, 0, 1), (2 * DH, 0, 1), (3 * DH, 1, 1), (4 * DH, 1, 1), (5 * DH, 2, 1)]
LOADS = 16 * (len(Q_RUNS) + len(K_RUNS))

ROUNDS = [(2, 0, 384, True), (1, 0, 256, True), (0, 0, 128, True), (3, 0, 512, True),
          (4, 0, 512, False), (5, 0, 512, False), (6, 0, 512, False), (6, 1, 384, True),
          (5, 1, 256, True), (4, 1, 128, True), (7, 0, 512, False), (7, 1, 512, True)]
UNITS = [(c, j, max(0, (j - CT * c) * P)) for c in range(HALVES) for j in range(CT * (c + 1))]
NU = len(UNITS)
PRING = 4
SLOT_USES = [2 * len(ROUNDS) + 1, 2 * len(ROUNDS)]
TURN_AFTER = 2


def program(nc, x, gamma, beta, wq, bq, wk, bk, wv, bv, wo, bo, wr, wkk, wvv, mu_r, mu_k, cos, sin, out):
    ctx = ExitStack()
    with ctx:
        scope = [ctx]

        def sb(name, shape, dt=F32):
            return scope[-1].enter_context(nc.sbuf_tensor(name, shape, dt))

        def plain_sem(name):
            return ctx.enter_context(nc.semaphore(name))

        counted = []

        def sem(name):
            counted.append(plain_sem(name))
            return counted[-1]

        def start_counters(sp):
            for s in counted:
                sp.sem_inc(s, START)
            counted.clear()

        def dram(name, shape, dt):
            return nc.dram_tensor(name, shape, dt, kind="Internal").ap()

        banks = [ctx.enter_context(nc.psum_tensor(f"bank{i}", [P, 2, CH], F32)) for i in range(4)]

        q_dram = dram("q_parts", [B, H, 3, 2, PAIR, L], BF16)
        k_dram = dram("k_parts", [B, H, 3, 2, PAIR, L], BF16)
        v_dram = dram("v_rows", [B, NG, P, NT, HG * DH], F32)
        attn_dram = dram("attn_rows", [B, NG, P, NT, HG * DH], F32)

        m_dram = dram("max_rows", [NG, SHIFT * HG * NT, P], BF16)

        x_rows = x.rearrange("b (c t p) d -> (b c) p t d", p=P, t=CT)
        out_rows = out.rearrange("b (c t p) d -> (b c) p t d", p=P, t=CT)

        ident = sb("ident", [P, P])
        ident16 = sb("ident16", [P, P], BF16)
        causal = sb("causal", [P, CH], BF16)
        cos_sb = sb("cos_sb", [P, L])
        sin_sb = sb("sin_sb", [P, L])
        w_sb = {n: sb(f"w_{n}", [P, KC, D]) for n in ("q", "k", "v", "o", "r", "kk", "vv")}
        col = sb("col", [P, 8, KC])
        bo_row = sb("bo_row", [1, D])
        ones_row = sb("ones_row", [1, P])
        bias_out = sb("bias_out", [P, D])
        epsc = sb("epsc", [P, CT])

        s_w = plain_sem("weights_loaded")
        s_wc = plain_sem("vectors_loaded")
        s_c = sem("constants_set")
        s_cq = sem("scaled_bias_set")
        s_bo = sem("output_bias_sum")


        scope.append(ExitStack())
        xa = sb("xa", [P, 2, CT, D])
        xn = sb("xn", [P, 2, CT, D])
        stats = sb("stats", [P, CT, 6])
        mv = sb("mv", [P, CT, 2])
        rstd = sb("rstd", [P, CT])
        vare = sb("vare", [P, CT])
        xnT = sb("xnT", [P, 2, KC, CH])
        proj = {n: sb(f"proj_{n}", [P, 2, CH]) for n in "qk"}
        mulc = {n: sb(f"mulc_{n}", [P, 2, CH]) for n in "qk"}
        muls = {n: sb(f"muls_{n}", [P, 2, CH]) for n in "qk"}
        rot = {n: sb(f"rot_{n}", [P, 2, CH]) for n in "qk"}
        rest = {n: sb(f"rest_{n}", [P, 2, CH]) for n in "qk"}
        parts = {n: sb(f"parts_{n}", [P, 2, 3, 2, CH], BF16) for n in "qk"}
        v_sb = sb("v_sb", [P, 2, NG, CT, HG * DH])

        a_x = [sem(f"a_x_loaded{u}") for u in range(2)]
        a_stat = sem("a_stats")
        a_mv = sem("a_mean_var")
        a_eps = sem("a_var_eps")
        a_rstd = sem("a_rstd")
        a_xn = sem("a_xn")
        a_T = sem("a_turned")
        a_xnT = sem("a_xnT")
        a_p = {n: sem(f"a_{n}_projected") for n in "qkv"}
        a_e = {n: sem(f"a_{n}_evacuated") for n in "qkv"}
        a_mul = {n: sem(f"a_{n}_products") for n in "qk"}
        a_rot = {n: sem(f"a_{n}_rotated") for n in "qk"}
        a_h = {n: sem(f"a_{n}_high") for n in "qk"}
        a_r1 = {n: sem(f"a_{n}_rest") for n in "qk"}
        a_m = {n: sem(f"a_{n}_middle") for n in "qk"}
        a_l = {n: sem(f"a_{n}_low") for n in "qk"}
        a_w = {n: [sem(f"a_{n}_written{u}") for u in range(2)] for n in "qkv"}
        NP16 = 16 * 6

        turn_bank, q_bank, k_bank, v_bank = banks
        chunks = B * HALVES

        with nc.Block() as block:
            def products(eng, n, i, u):
                eng.wait_ge(a_e[n], START + i + 1)
                eng.wait_ge(a_rot[n], START + i)
                for table, dst in ((cos_sb, mulc[n]), (sin_sb, muls[n])):
                    t = table[:, u * CH:(u + 1) * CH].unsqueeze(1).to_broadcast([P, 2, CH])
                    eng.tensor_tensor(dst[:, :, :], proj[n][:, :, :], t, ALU.mult).then_inc(a_mul[n], 1)

            @block.sync
            def _(sp):
                for n, w in (("q", wq), ("k", wk), ("v", wv), ("o", wo), ("r", wr), ("kk", wkk), ("vv", wvv)):
                    sp.dma_start(w_sb[n][:, :, :], w.rearrange("(k p) n -> p k n", p=P)).then_inc(s_w, 16)
                sp.dma_start(cos_sb[:, :], cos).then_inc(s_w, 16)
                sp.dma_start(sin_sb[:, :], sin).then_inc(s_w, 16)
                sp.dma_start(bo_row[:, :], bo.rearrange("(o d) -> o d", o=1)).then_inc(s_w, 16)
                start_counters(sp)
                for u in range(2):
                    sp.dma_start(xa[:, u], x_rows[u]).then_inc(a_x[u], 16)
                sp.wait_ge(a_xn, START + 1)
                sp.dma_start(xa[:, 0], x_rows[2]).then_inc(a_x[0], 16)
                with sp.Fori(0, B) as b:
                    for u in range(2):
                        i = b * 2 + u
                        sp.wait_ge(a_xn, START + i + 2)
                        sp.nop(nofuse=True)
                        sp.dma_start(xa[:, 1 - u], x_rows[(i + 3) & (chunks - 1)]).then_inc(a_x[1 - u], 16)
                        toks = slice(u * CH, (u + 1) * CH)
                        sp.wait_ge(a_e["v"], START + i + 1)
                        sp.nop(nofuse=True)
                        sp.dma_start(v_dram[b, :, :, u * CT:(u + 1) * CT, :].rearrange("g p t d -> p g (t d)"),
                                     v_sb[:, u].rearrange("p g t d -> p g (t d)")).then_inc(a_w["v"][u], 16)
                        for n, dst in (("k", k_dram), ("q", q_dram)):
                            sp.wait_ge(a_l[n], START + i + 1)
                            sp.nop(nofuse=True)
                            for part in range(3):
                                for c in range(2):
                                    sp.dma_start(dst[b, :, part, c, :, toks],
                                                 parts[n][:, u, part, c, :]).then_inc(a_w[n][u], 16)
                for u in range(2):
                    sp.wait_ge(a_x[u], START + 16 * (B + 2 - u))
                    sp.nop(nofuse=True)
                    sp.wait_ge(a_w["v"][u], START + 16 * B)
                    sp.nop(nofuse=True)
                    sp.wait_ge(a_w["q"][u], START + NP16 * B)
                    sp.nop(nofuse=True)
                    sp.wait_ge(a_w["k"][u], START + NP16 * B)
                    sp.nop(nofuse=True)

            @block.gpsimd
            def _(pool):
                c = [0]

                def link(ins):
                    c[0] += 1
                    ins.then_inc(s_c, 1)
                    pool.wait_ge(s_c, START + c[0])

                link(pool.memset(ident[:, :], 0.0))
                link(pool.affine_select(out=ident[:, :], in_=ident[:, :], compare_op=ALU.not_equal, fill=1.0,
                                        base=0, pattern=[[-1, P]], channel_multiplier=1))
                link(pool.tensor_copy(ident16[:, :], ident[:, :]))
                link(pool.memset(causal[:, :], 0.0))
                link(pool.affine_select(out=causal[:, CH - P:], in_=causal[:, CH - P:], compare_op=ALU.is_ge,
                                        fill=LOWEST, base=0, pattern=[[-1, P]], channel_multiplier=1))
                link(pool.memset(epsc[:, :], -0.5))
                link(pool.memset(ones_row[:, :], 1.0))
                for n, v in enumerate((gamma, beta, bq, bk, bv, mu_r, mu_k)):
                    with nc.allow_non_contiguous_dma(reason="256 values in all"):
                        pool.dma_start(col[:, n, :], v.rearrange("(k p) -> p k", p=P)).then_inc(s_wc, 16)
                pool.wait_ge(s_w, 16 * 10)
                pool.wait_ge(s_wc, 16 * 7)
                pool.tensor_scalar(col[:, 7, :], col[:, 2, :], 0.25, 0.0, ALU.mult, ALU.add).then_inc(s_cq, 1)

                def chunk_rstd(i):
                    pool.wait_ge(a_mv, START + i + 1)
                    pool.nop(nofuse=True)
                    pool.tensor_scalar(vare[:, :], mv[:, :, 1], EPS, 1.0, ALU.add, ALU.mult).then_inc(a_eps, 1)
                    pool.wait_ge(a_eps, START + i + 1)
                    pool.tensor_tensor(rstd[:, :], vare[:, :], epsc[:, :], ALU.pow).then_inc(a_rstd, 1)

                chunk_rstd(0)
                chunk_rstd(1)
                with pool.Fori(0, B) as b:
                    for u in range(2):
                        i = b * 2 + u
                        products(pool, "k", i, u)
                        chunk_rstd(i + 2)
                        pool.wait_ge(a_h["k"], START + i + 1)
                        pool.wait_ge(a_m["k"], START + i)
                        pool.wait_ge(a_l["k"], START + i)
                        pool.tensor_tensor(rest["k"][:, :, :], rot["k"][:, :, :], parts["k"][:, u, 0], ALU.subtract)\
                            .then_inc(a_r1["k"], 1)

            @block.vector
            def _(dve):
                def chunk_stats(i, u, loads):
                    dve.wait_ge(a_x[u], START + loads)
                    for t in range(CT):
                        ins = dve.bn_stats(stats[:, t, :], xa[:, u, t, :])
                    ins.then_inc(a_stat, 1)
                    dve.wait_ge(a_stat, START + i + 1)
                    dve.nop(nofuse=True)
                    for t in range(CT):
                        ins = dve.bn_aggr(mv[:, t, :], stats[:, t, :])
                    ins.then_inc(a_mv, 1)

                def normalise(i, u):
                    dve.wait_ge(a_rstd, START + i + 1)
                    dve.wait_ge(a_mv, START + i + 1)
                    if not isinstance(i, int):
                        dve.wait_ge(a_T, START + i - 1)
                    for t in range(CT):
                        ins = dve.tensor_scalar(xn[:, u, t, :], xa[:, u, t, :], mv[:, t, 0:1], rstd[:, t:t + 1],
                                                ALU.subtract, ALU.mult)
                    ins.then_inc(a_xn, 1)

                def rotate(n, i):
                    dve.wait_ge(a_mul[n], START + 2 * i + 2)
                    dve.wait_ge(a_h[n], START + i)
                    dve.wait_ge(a_r1[n], START + i)
                    dve.tensor_tensor(rot[n][:, 0, :], mulc[n][:, 0, :], muls[n][:, 1, :], ALU.subtract)
                    dve.tensor_tensor(rot[n][:, 1, :], muls[n][:, 0, :], mulc[n][:, 1, :],
                                      ALU.add).then_inc(a_rot[n], 1)

                def rest_q(i, u):
                    dve.wait_ge(a_h["q"], START + i + 1)
                    dve.wait_ge(a_m["q"], START + i)
                    dve.tensor_tensor(rest["q"][:, :, :], rot["q"][:, :, :], parts["q"][:, u, 0], ALU.subtract)\
                       .then_inc(a_r1["q"], 1)

                def low_part(n, i, u):
                    dve.wait_ge(a_m[n], START + i + 1)
                    dve.wait_ge(a_r1[n], START + i + 1)
                    dve.tensor_tensor(parts[n][:, u, 2], rest[n][:, :, :], parts[n][:, u, 1], ALU.subtract)\
                       .then_inc(a_l[n], 1)

                chunk_stats(0, 0, 16)
                normalise(0, 0)
                chunk_stats(1, 1, 16)
                with dve.Fori(0, B) as b:
                    for u in range(2):
                        i = b * 2 + u
                        normalise(i + 1, 1 - u)
                        chunk_stats(i + 2, u, 16 * b + 32)
                        products(dve, "q", i, u)
                        rotate("k", i)
                        rotate("q", i)
                        rest_q(i, u)
                        low_part("k", i, u)
                        low_part("q", i, u)

            @block.scalar
            def _(act):
                def turn_out(i, u, first):
                    act.wait_ge(a_T, START + i + 1)
                    if not first:
                        act.wait_ge(a_p["v"], START + i - 1)
                    for k in range(KC):
                        ins = act.activation(xnT[:, u, k, :], turn_bank[:, k, :], ACT.Identity,
                                             bias=col[:, 1, k:k + 1], scale=col[:, 0, k:k + 1])
                    ins.then_inc(a_xnT, 1)

                def project_out(n, i):
                    act.wait_ge(a_p[n], START + i + 1)
                    act.wait_ge(a_mul[n], START + 2 * i)
                    bank, scale, bias = (q_bank, 0.25, 7) if n == "q" else (k_bank, 1.0, 3)
                    for c in range(2):
                        ins = act.activation(proj[n][:, c, :], bank[:, c, :], ACT.Identity,
                                             bias=col[:, bias, c:c + 1], scale=scale)
                    ins.then_inc(a_e[n], 1)

                def high(n, i, b, u):
                    act.wait_ge(a_rot[n], START + i + 1)
                    act.wait_ge(a_w[n][u], START + NP16 * b)
                    act.activation(parts[n][:, u, 0], rot[n][:, :, :], ACT.Identity).then_inc(a_h[n], 1)

                def middle(n, i, u):
                    act.wait_ge(a_r1[n], START + i + 1)
                    act.activation(parts[n][:, u, 1], rest[n][:, :, :], ACT.Identity).then_inc(a_m[n], 1)

                act.wait_ge(s_w, 16 * 10)
                act.wait_ge(s_wc, 16 * 7)
                act.wait_ge(s_cq, START + 1)
                turn_out(0, 0, True)
                with act.Fori(0, B) as b:
                    for u in range(2):
                        i = b * 2 + u
                        project_out("k", i)
                        project_out("q", i)
                        turn_out(i + 1, 1 - u, False)
                        high("k", i, b, u)
                        high("q", i, b, u)
                        act.wait_ge(a_p["v"], START + i + 1)
                        act.wait_ge(a_w["v"][u], START + 16 * b)
                        for t2 in range(2):
                            ins = act.activation(
                                v_sb[:, u, :, 2 * t2:2 * t2 + 2, :],
                                v_bank[:, t2, :].rearrange("p (t g d) -> p g t d", t=2, g=NG), ACT.Identity)
                        ins.then_inc(a_e["v"], 1)
                        middle("k", i, u)
                        middle("q", i, u)

            @block.tensor
            def _(pe):
                def turn(i, u):
                    pe.wait_ge(a_xn, START + i + 1)
                    pe.wait_ge(a_xnT, START + i)
                    for k in range(KC):
                        for t in range(CT):
                            ins = pe.transpose(turn_bank[:, k, t * P:(t + 1) * P],
                                               xn[:, u, t, k * P:(k + 1) * P], ident[:, :])
                    ins.then_inc(a_T, 1)

                def project(n, i, u):
                    pe.wait_ge(a_xnT, START + i + 1)
                    pe.wait_ge(a_e[n], START + i)
                    bank = q_bank if n == "q" else k_bank
                    for c in range(2):
                        for k in range(KC):
                            ins = pe.matmul(bank[:, c, :], w_sb[n][:, k, c * P:(c + 1) * P], xnT[:, u, k, :],
                                            start=(k == 0), stop=(k == KC - 1))
                    ins.then_inc(a_p[n], 1)

                def project_v(i, u):
                    pe.wait_ge(a_e["v"], START + i)
                    for t in range(CT):
                        for k in range(KC):
                            ins = pe.matmul(v_bank[:, t // 2, (t % 2) * D:(t % 2 + 1) * D],
                                            xnT[:, u, k, t * P:(t + 1) * P], w_sb["v"][:, k, :],
                                            start=(k == 0), stop=(k == KC - 1))
                    ins.then_inc(a_p["v"], 1)

                pe.wait_ge(s_w, 16 * 10)
                pe.wait_ge(s_wc, 16 * 7)
                pe.wait_ge(s_c, START + 7)
                turn(0, 0)
                with pe.Fori(0, B) as b:
                    for u in range(2):
                        i = b * 2 + u
                        project("k", i, u)
                        project("q", i, u)
                        turn(i + 1, 1 - u)
                        project_v(i, u)

        scope.pop().close()

        scope.append(ExitStack())
        q_st = [sb(f"q_stack{g}", [P, HG, L], BF16) for g in range(NG)]
        k_st = [sb(f"k_stack{g}", [P, HG, L], BF16) for g in range(NG)]
        v_ld = [sb(f"v_loaded{g}", [P, NT, HG * DH]) for g in range(NG)]
        v_pad = [sb(f"v_padded{g}", [P, NT, HG, VW]) for g in range(NG)]
        probs = sb("probs", [P, PRING, HG, CH])
        junk = sb("junk", [P, 2, CH], BF16)
        mx = sb("mx", [P, 2, HG, NT])
        mrow = sb("mrow", [P, HG * NT])
        mrest = sb("mrest", [P, HG * NT])
        mparts = sb("mparts", [P, SHIFT, HG * NT], BF16)
        mturn = sb("mturn", [SHIFT * HG * NT, P], BF16)
        osum = sb("osum", [P, HALVES, CH])
        orec = sb("orec", [P, HALVES, CT * HG])
        oattn = sb("oattn", [P, HALVES, CT, HG * DH])

        b_init = sem("b_buffers_set")
        b_ld = [sem(f"b_stack_loaded{g}") for g in range(NG)]
        b_vld = [sem(f"b_v_loaded{g}") for g in range(NG)]
        b_v = sem("b_v_padded")
        b_s1 = [sem(f"b_scores1_done{s}") for s in range(2)]
        b_f1 = [sem(f"b_scores1_used{s}") for s in range(2)]
        b_rnd = sem("b_rounds_reduced")
        b_mc = sem("b_max_steps")
        b_mrow = [sem(f"b_max_rows_loaded{g}") for g in range(NG)]
        b_mw = sem("b_max_written")
        b_st = [sem(f"b_scores2_done{s}") for s in range(2)]
        b_ex = [sem(f"b_exp_done{s}") for s in range(2)]
        b_sel = sem("b_diagonal_cut")
        b_pv = [sem(f"b_pv_done{s}") for s in range(PRING)]
        b_os = [sem(f"b_sums_out{c}") for c in range(HALVES)]
        b_ot = [sem(f"b_sums_turned{c}") for c in range(HALVES)]
        b_rc = [sem(f"b_reciprocal{c}") for c in range(HALVES)]
        b_nm = [sem(f"b_normalised{c}") for c in range(HALVES)]
        b_aw = [sem(f"b_attn_written{c}") for c in range(HALVES)]
        MSTEPS = 5
        UPR = NU // PRING

        s1_bank = banks[0]
        s2_bank = [banks[1], banks[2]]
        acc = banks[3]
        pass1_diag = [r for r, rd in enumerate(ROUNDS) if rd[3]]
        diag_units = [u for u, (c, j, o) in enumerate(UNITS) if j // CT == c]

        with nc.Block() as block:
            @block.sync
            def _(sp):
                def load(g, b):
                    for st, src, runs in ((q_st[g], q_dram, Q_RUNS), (k_st[g], k_dram, K_RUNS)):
                        heads = src[b, g * HG:(g + 1) * HG].rearrange("h a c r n -> (a c r) h n")
                        for row, part, n in runs:
                            sp.dma_start(st[row:row + n * DH, :, :],
                                         heads[part * DH:(part + n) * DH]).then_inc(b_ld[g], 16)
                    sp.dma_start(v_ld[g][:, :, :], v_dram[b, g]).then_inc(b_vld[g], 16)

                def load_max_rows(g, p):
                    sp.wait_ge(b_f1[0], START + SLOT_USES[0] * p + 2 * TURN_AFTER + 3)
                    sp.nop(nofuse=True)
                    sp.dma_start(m_dram[g], mturn[:, :]).then_inc(b_mw, 16)
                    sp.wait_ge(b_mw, START + 16 * p)
                    sp.nop(nofuse=True)
                    sp.dma_start(q_st[g][STACK:STACK + SHIFT].rearrange("s h t -> s (h t)"),
                                 m_dram[g].rearrange("(s r) n -> s (r n)", s=SHIFT)).then_inc(b_mrow[g], 16)

                start_counters(sp)
                for g in range(3):
                    load(g, 0)
                load_max_rows(0, 1)
                with sp.Fori(0, B) as b:
                    nb = (b + 1) & (B - 1)
                    for g in range(NG):
                        n = b * NG + g
                        sp.wait_ge(b_st[1], START + NU * n)
                        sp.nop(nofuse=True)
                        sp.wait_ge(b_pv[PRING - 1], START + UPR * n)
                        sp.nop(nofuse=True)
                        load((g + 3) % NG, b if g == 0 else nb)
                        load_max_rows((g + 1) % NG, n + 2)
                        for c in range(HALVES):
                            sp.wait_ge(b_nm[c], START + n + 1)
                            sp.nop(nofuse=True)
                            sp.dma_start(attn_dram[b, g, :, c * CT:(c + 1) * CT, :], oattn[:, c])\
                              .then_inc(b_aw[c], 16)
                for c in range(HALVES):
                    sp.wait_ge(b_aw[c], START + 16 * B * NG)
                    sp.nop(nofuse=True)
                for g in range(NG):
                    loads = B + 1 if g < 3 else B
                    sp.wait_ge(b_ld[g], START + LOADS * loads)
                    sp.nop(nofuse=True)
                    sp.wait_ge(b_vld[g], START + 16 * loads)
                    sp.nop(nofuse=True)
                sp.wait_ge(b_mrow[0], START + 16 * (B + 1))

            @block.gpsimd
            def _(pool):
                for g in range(NG):
                    pool.memset(v_pad[g][:, :, :, DH:], 1.0)
                pool.memset(mparts[:, :, :], 0.0).then_inc(b_init, 1)

                def pad_v(g, loads):
                    pool.wait_ge(b_vld[g], START + 16 * loads)
                    pool.nop(nofuse=True)
                    pool.tensor_scalar(v_pad[g][:, :, :, 0:DH],
                                       v_ld[g][:, :, :].rearrange("p t (h d) -> p t h d", h=HG),
                                       1.0, 1.0, ALU.mult, ALU.mult).then_inc(b_v, 1)

                for g in range(3):
                    pad_v(g, 1)
                with pool.Fori(0, B) as b:
                    for g in range(NG):
                        n = b * NG + g
                        for u in diag_units:
                            for s in range(2):
                                pool.wait_ge(b_ex[s], START + NU * n + u + 1)
                                pool.nop(nofuse=True)
                            tile = probs[:, u % PRING, :, 0:P]
                            pool.affine_select(out=tile, in_=tile, compare_op=ALU.is_ge, fill=0.0, base=0,
                                               pattern=[[0, HG], [1, P]], channel_multiplier=-1)\
                                .then_inc(b_sel, 1)
                        pad_v((g + 3) % NG, b + 1 if g == 0 else b + 2)

            @block.vector
            def _(dve):
                def take_maxima(m, normal):
                    uses = [0, 0]
                    for r, (t, half, w, masked) in enumerate(ROUNDS):
                        for h in range(HG):
                            s = h % 2
                            dve.wait_ge(b_s1[s], START + m * SLOT_USES[s] + uses[s] + 1)
                            dve.nop(nofuse=True)
                            uses[s] += 1
                            dst = mx[:, half, h, t:t + 1]
                            if masked:
                                dve.tensor_tensor_reduce(junk[:, s, 0:w], s1_bank[:, s, 0:w], causal[:, CH - w:],
                                                         1.0, LOWEST, ALU.add, ALU.max, dst)\
                                   .then_inc(b_f1[s], 1)
                            else:
                                dve.tensor_reduce(dst, s1_bank[:, s, 0:w], AX.X, ALU.max).then_inc(b_f1[s], 1)
                        if r == TURN_AFTER:
                            dve.wait_ge(b_s1[0], START + m * SLOT_USES[0] + uses[0] + 1)
                            uses[0] += 1
                            dve.tensor_copy(mturn[:, :], s1_bank[0:SHIFT * HG * NT, 0, 0:P // 2].bitcast(BF16))\
                               .then_inc(b_f1[0], 1)
                        if normal is not None and r == 8:
                            normal(0)
                    step = [0]

                    def link(ins):
                        step[0] += 1
                        ins.then_inc(b_mc, 1)
                        dve.wait_ge(b_mc, START + m * MSTEPS + step[0])

                    dve.wait_ge(b_f1[0], START + m * SLOT_USES[0] + uses[0] - 1)
                    dve.wait_ge(b_f1[1], START + m * SLOT_USES[1] + uses[1])
                    flat = [mx[:, k].rearrange("p h t -> p (h t)") for k in range(2)]
                    link(dve.tensor_tensor(mrow[:, :], flat[0], flat[1], ALU.max))
                    link(dve.tensor_scalar(mparts[:, 0], mrow[:, :], -1.0, None, ALU.mult))
                    link(dve.scalar_tensor_tensor(out=mrest[:, :], in0=mrow[:, :], scalar=-1.0, in1=mparts[:, 0],
                                                  op0=ALU.mult, op1=ALU.subtract))
                    link(dve.tensor_copy(mparts[:, 1], mrest[:, :]))
                    link(dve.tensor_tensor(mparts[:, 2], mrest[:, :], mparts[:, 1], ALU.subtract))
                    if normal is not None:
                        normal(1)

                dve.memset(mx[:, 1, :, 0:CT], LOWEST)
                for g in range(NG):
                    dve.memset(k_st[g][STACK:STACK + SHIFT], 1.0).then_inc(b_init, 1)
                take_maxima(0, None)
                take_maxima(1, None)
                with dve.Fori(0, B) as b:
                    for g in range(NG):
                        n = b * NG + g

                        def normal(c):
                            turned = acc[:, c, :].rearrange("p (s w) -> p s w", w=VW)
                            dve.wait_ge(b_ot[c], START + n + 1)
                            dve.reciprocal(orec[:, c, :], turned[:, :, DH]).then_inc(b_rc[c], 1)
                            dve.wait_ge(b_rc[c], START + n + 1)
                            dve.wait_ge(b_aw[c], START + 16 * n)
                            dve.tensor_tensor(oattn[:, c].rearrange("p t (h d) -> p (t h) d", h=HG),
                                              turned[:, :, 0:DH],
                                              orec[:, c, :].unsqueeze(2).to_broadcast([P, CT * HG, DH]),
                                              ALU.mult).then_inc(b_nm[c], 1)

                        take_maxima(n + 2, normal)

            @block.scalar
            def _(act):
                def sums_out(c, n):
                    act.wait_ge(b_pv[PRING - 1], START + (UPR * n + (1 if c == 0 else UPR)))
                    act.wait_ge(b_ot[c], START + n)
                    act.activation(osum[:, c, :], acc[:, c, :], ACT.Identity).then_inc(b_os[c], 1)

                with act.Fori(0, B) as b:
                    for g in range(NG):
                        n = b * NG + g
                        for u, (c, j, o) in enumerate(UNITS):
                            act.wait_ge(b_pv[u % PRING], START + UPR * n + u // PRING)
                            for s in range(2):
                                act.wait_ge(b_st[s], START + NU * n + u + 1)
                                act.activation(probs[:, u % PRING, 2 * s:2 * s + 2, 0:CH - o],
                                               s2_bank[s][:, :, 0:CH - o], ACT.Exp).then_inc(b_ex[s], 1)
                            if u == 5:
                                sums_out(0, n)
                        sums_out(1, n)

            @block.tensor
            def _(pe):
                def pass1(m, g, r, heads, uses):
                    t, half, w, _ = ROUNDS[r]
                    for h in heads:
                        s = h % 2
                        pe.wait_ge(b_f1[s], START + m * SLOT_USES[s] + uses[s])
                        pe.matmul(s1_bank[:, s, 0:w], q_st[g][0:STACK, h, t * P:(t + 1) * P],
                                  k_st[g][0:STACK, h, half * CH:half * CH + w],
                                  start=True, stop=True).then_inc(b_s1[s], 1)
                        uses[s] += 1

                def turn_max(m, uses):
                    pe.wait_ge(b_f1[0], START + m * SLOT_USES[0] + uses[0])
                    pe.wait_ge(b_mc, START + m * MSTEPS)
                    pe.transpose(s1_bank[0:SHIFT * HG * NT, 0, 0:P // 2].bitcast(BF16),
                                 mparts[:, :, :].rearrange("p s n -> p (s n)"), ident16[:, :])\
                      .then_inc(b_s1[0], 1)
                    uses[0] += 1

                pe.wait_ge(b_init, START + 1 + NG)
                for m in range(2):
                    pe.wait_ge(b_ld[m], START + LOADS)
                    uses = [0, 0]
                    for r in range(len(ROUNDS)):
                        pass1(m, m, r, range(HG), uses)
                        if r == TURN_AFTER:
                            turn_max(m, uses)

                with pe.Fori(0, B) as b:
                    for g in range(NG):
                        n = b * NG + g
                        g1 = (g + 2) % NG
                        uses = [0, 0]

                        def scores2(u, s):
                            c, j, o = UNITS[u]
                            pe.wait_ge(b_ex[s], START + NU * n + u)
                            for h in (2 * s, 2 * s + 1):
                                ins = pe.matmul(s2_bank[s][:, h % 2, 0:CH - o],
                                                k_st[g][0:STACK + SHIFT, h, j * P:(j + 1) * P],
                                                q_st[g][0:STACK + SHIFT, h, c * CH + o:(c + 1) * CH],
                                                start=True, stop=True)
                            ins.then_inc(b_st[s], 1)

                        def pv(u):
                            c, j, o = UNITS[u]
                            if j == 0:
                                pe.wait_ge(b_nm[c], START + n)
                            for s in range(2):
                                pe.wait_ge(b_ex[s], START + NU * n + u + 1)
                            if u in diag_units:
                                pe.wait_ge(b_sel, START + len(diag_units) * n + diag_units.index(u) + 1)
                            for h in range(HG):
                                ins = pe.matmul(acc[32 * h:32 * h + VW, c, o:CH], v_pad[g][:, j, h, :],
                                                probs[:, u % PRING, h, 0:CH - o],
                                                start=(j == 0), stop=(j == CT * (c + 1) - 1),
                                                skip_group_check=True)
                            ins.then_inc(b_pv[u % PRING], 1)

                        def turn_sums(c):
                            pe.wait_ge(b_os[c], START + n + 1)
                            for t in range(CT):
                                ins = pe.transpose(acc[:, c, t * P:(t + 1) * P], osum[:, c, t * P:(t + 1) * P],
                                                   ident[:, :])
                            ins.then_inc(b_ot[c], 1)

                        pe.wait_ge(b_ld[g1], START + (LOADS * (b + 1) if g < 2 else LOADS * (b + 2)))
                        pe.wait_ge(b_mrow[g], START + 16 * (b + 1))
                        pe.wait_ge(b_v, START + n + 1)
                        m = n + 2
                        for u in range(NU):
                            scores2(u, 0)
                            if u < 10:
                                pass1(m, g1, u, (0, 1), uses)
                            scores2(u, 1)
                            if u < 10:
                                pass1(m, g1, u, (2, 3), uses)
                            if u == TURN_AFTER:
                                turn_max(m, uses)
                            if u >= 10:
                                pass1(m, g1, 10, ((0, 1), (2, 3))[u - 10], uses)
                            if u >= 1:
                                pv(u - 1)
                            if u == 7:
                                turn_sums(0)
                        pass1(m, g1, 11, (0, 1), uses)
                        pv(NU - 1)
                        pass1(m, g1, 11, (2, 3), uses)
                        turn_sums(1)

        scope.pop().close()

        scope.append(ExitStack())
        x_c = sb("x_c", [P, 2, CT, D])
        at = sb("at", [P, 2, CT, D])
        atT = sb("atT", [P, KC, CH])
        x2b = sb("x2b", [P, CT, D])
        x2 = sb("x2", [P, CT, D])
        y = sb("y", [P, CT, D])
        y1 = sb("y1", [P, 2, CT, D])
        y1T = sb("y1T", [P, KC, CH + 1])
        dx = sb("dx", [P, KC, CH])
        xr = sb("xr", [P, 2, KC, CH])
        xk = sb("xk", [P, 2, KC, CH])
        r_sb = sb("r_sb", [P, CT, D])
        kr = sb("kr", [P, KC, CH])
        ka = sb("ka", [P, KC, CH])
        ff = sb("ff", [P, CT, D])
        z = sb("z", [P, CT, D])
        zo = sb("zo", [P, 2, CT, D])
        st1 = sb("st1", [P, CT, 6])
        mv1 = sb("mv1", [P, CT, 2])
        ve1 = sb("ve1", [P, CT])
        rs1 = sb("rs1", [P, CT])
        st2 = sb("st2", [P, CT, 6])
        mv2 = sb("mv2", [P, CT, 2])
        ve2 = sb("ve2", [P, CT])
        rs2 = sb("rs2", [P, CT])

        names = ["x2", "x2b", "aT", "atT", "o", "y", "st1", "mv1", "ve1", "rs1", "y1", "yT", "y1T", "carry", "dx",
                 "xk", "xr", "r", "r_sb", "k", "kr", "ka", "kv", "ff", "z", "st2", "mv2", "ve2", "rs2"]
        c_x = [sem(f"c_x_loaded{u}") for u in range(2)]
        c_at = [sem(f"c_attn_loaded{u}") for u in range(2)]
        c_out = [sem(f"c_written{u}") for u in range(2)]
        c_zo = sem("c_zo")
        c = {n: sem(f"c_{n}") for n in names}
        T_bank, N_bank, R_bank, K_bank = banks

        with nc.Block() as block:
            @block.sync
            def _(sp):
                def load_x(i, u):
                    sp.dma_start(x_c[:, u], x_rows[i]).then_inc(c_x[u], 16)

                def load_attn(b, u):
                    for g in range(NG):
                        sp.dma_start(at[:, u, :, g * HG * DH:(g + 1) * HG * DH],
                                     attn_dram[b, g, :, u * CT:(u + 1) * CT, :]).then_inc(c_at[u], 16)

                start_counters(sp)
                for u in range(2):
                    load_attn(0, u)
                    load_x(u, u)
                for u in range(2):
                    sp.wait_ge(c["aT"], START + u + 1)
                    load_attn(1, u)
                    sp.wait_ge(c["x2"], START + u + 1)
                    load_x(u + 2, u)
                with sp.Fori(0, B) as b:
                    for u in range(2):
                        i = b * 2 + u
                        sp.wait_ge(c["aT"], START + i + 3)
                        sp.nop(nofuse=True)
                        load_attn((b + 2) & (B - 1), u)
                        sp.wait_ge(c["x2"], START + i + 3)
                        sp.nop(nofuse=True)
                        load_x((i + 4) & (chunks - 1), u)
                        sp.wait_ge(c_zo, START + i + 1)
                        sp.nop(nofuse=True)
                        sp.dma_start(out_rows[i], zo[:, u]).then_inc(c_out[u], 16)
                for u in range(2):
                    sp.wait_ge(c_out[u], START + 16 * B)
                    sp.nop(nofuse=True)
                    sp.wait_ge(c_x[u], START + 16 * (B + 2))
                    sp.nop(nofuse=True)
                    sp.wait_ge(c_at[u], START + 16 * NG * (B + 2))
                    sp.nop(nofuse=True)

            def rsqrt(eng, i, tag, mvt, vet, rst):
                eng.wait_ge(c["mv" + tag], START + i + 1)
                eng.nop(nofuse=True)
                eng.tensor_scalar(vet[:, :], mvt[:, :, 1], EPS, 1.0, ALU.add, ALU.mult).then_inc(c["ve" + tag], 1)
                eng.wait_ge(c["ve" + tag], START + i + 1)
                eng.tensor_tensor(rst[:, :], vet[:, :], epsc[:, :], ALU.pow).then_inc(c["rs" + tag], 1)

            @block.gpsimd
            def _(pool):
                def residual(i, u, b):
                    pool.wait_ge(c_x[u], START + 16 * b + 16)
                    pool.nop(nofuse=True)
                    pool.wait_ge(c["y"], START + i)
                    pool.nop(nofuse=True)
                    pool.tensor_scalar(x2[:, :, :], x_c[:, u], 2.0, 1.0, ALU.mult, ALU.mult).then_inc(c["x2"], 1)
                    pool.wait_ge(c["x2"], START + i + 1)
                    pool.tensor_tensor(x2b[:, :, :], x2[:, :, :],
                                       bias_out[:, :].unsqueeze(1).to_broadcast([P, CT, D]), ALU.add)\
                        .then_inc(c["x2b"], 1)

                pool.wait_ge(s_bo, START + 2)
                residual(0, 0, 0)
                rsqrt(pool, 0, "1", mv1, ve1, rs1)
                residual(1, 1, 0)
                rsqrt(pool, 1, "1", mv1, ve1, rs1)
                with pool.Fori(0, B) as b:
                    for u in range(2):
                        i = b * 2 + u
                        residual(i + 2, u, b + 1)
                        pool.wait_ge(c["ff"], START + i + 1)
                        pool.tensor_tensor(z[:, :, :], ff[:, :, :], y1[:, u], ALU.add).then_inc(c["z"], 1)
                        rsqrt(pool, i + 2, "1", mv1, ve1, rs1)
                        rsqrt(pool, i, "2", mv2, ve2, rs2)

            @block.vector
            def _(dve):
                def stats_of(src, i, tag, stt, mvt):
                    for t in range(CT):
                        ins = dve.bn_stats(stt[:, t, :], src[:, t, :])
                    ins.then_inc(c["st" + tag], 1)
                    dve.wait_ge(c["st" + tag], START + i + 1)
                    dve.nop(nofuse=True)
                    dve.wait_ge(c["rs" + tag], START + i)
                    dve.nop(nofuse=True)
                    for t in range(CT):
                        ins = dve.bn_aggr(mvt[:, t, :], stt[:, t, :])
                    ins.then_inc(c["mv" + tag], 1)

                def front(i):
                    dve.wait_ge(c["x2b"], START + i + 1)
                    dve.wait_ge(c["o"], START + i + 1)
                    for h in range(2):
                        ins = dve.tensor_tensor(
                            y[:, 2 * h:2 * h + 2, :], N_bank[:, h, :].rearrange("p (t d) -> p t d", d=D),
                            x2b[:, 2 * h:2 * h + 2, :], ALU.add)
                    ins.then_inc(c["y"], 1)
                    dve.wait_ge(c["y"], START + i + 1)
                    stats_of(y, i, "1", st1, mv1)

                def normal1(i, u, batch_start):
                    dve.wait_ge(c["xr"], START + i)
                    if batch_start:
                        dve.memset(y1T[:, :, 0:1], 0.0).then_inc(c["carry"], 1)
                    else:
                        dve.tensor_copy(y1T[:, :, 0:1], y1T[:, :, CH:CH + 1]).then_inc(c["carry"], 1)
                    dve.wait_ge(c["rs1"], START + i + 1)
                    dve.wait_ge(c["mv1"], START + i + 1)
                    for t in range(CT):
                        ins = dve.tensor_scalar(y1[:, u, t, :], y[:, t, :], mv1[:, t, 0:1], rs1[:, t:t + 1],
                                                ALU.subtract, ALU.mult)
                    ins.then_inc(c["y1"], 1)

                def mix(i, u):
                    dve.wait_ge(c["y1T"], START + i + 1)
                    dve.wait_ge(c["carry"], START + i + 1)
                    dve.tensor_tensor(dx[:, :, :], y1T[:, :, 1:], y1T[:, :, 0:CH], ALU.subtract)\
                       .then_inc(c["dx"], 1)
                    dve.wait_ge(c["dx"], START + i + 1)
                    for mu, dst, done in ((6, xk, "xk"), (5, xr, "xr")):
                        for k in range(KC):
                            ins = dve.scalar_tensor_tensor(out=dst[:, u, k, :], in0=dx[:, k, :],
                                                           scalar=col[:, mu, k:k + 1], in1=y1T[:, k, 0:CH],
                                                           op0=ALU.mult, op1=ALU.add)
                        ins.then_inc(c[done], 1)

                dve.wait_ge(s_bo, START + 1)
                dve.tensor_copy(bias_out[:, :], N_bank[:, 1, 0:D]).then_inc(s_bo, 1)
                front(0)
                normal1(0, 0, True)
                front(1)
                mix(0, 0)
                normal1(1, 1, False)
                with dve.Fori(0, B) as b:
                    for u in range(2):
                        i = b * 2 + u
                        dve.wait_ge(c["kv"], START + i + 1)
                        dve.wait_ge(c["r_sb"], START + i + 1)
                        for h in range(2):
                            ins = dve.tensor_tensor(
                                ff[:, 2 * h:2 * h + 2, :], N_bank[:, h, :].rearrange("p (t d) -> p t d", d=D),
                                r_sb[:, 2 * h:2 * h + 2, :], ALU.mult)
                        ins.then_inc(c["ff"], 1)
                        mix(i + 1, 1 - u)
                        front(i + 2)
                        dve.wait_ge(c["z"], START + i + 1)
                        stats_of(z, i, "2", st2, mv2)
                        normal1(i + 2, u, u == 0)
                        dve.wait_ge(c["rs2"], START + i + 1)
                        dve.wait_ge(c["mv2"], START + i + 1)
                        dve.wait_ge(c_out[u], START + 16 * b)
                        for t in range(CT):
                            ins = dve.tensor_scalar(zo[:, u, t, :], z[:, t, :], mv2[:, t, 0:1], rs2[:, t:t + 1],
                                                    ALU.subtract, ALU.mult)
                        ins.then_inc(c_zo, 1)

            @block.scalar
            def _(act):
                def front(i):
                    act.wait_ge(c["aT"], START + i + 1)
                    act.wait_ge(c["o"], START + i)
                    for k in range(KC):
                        ins = act.activation(atT[:, k, :], K_bank[:, k, :], ACT.Identity)
                    ins.then_inc(c["atT"], 1)

                def turn_out(i):
                    act.wait_ge(c["yT"], START + i + 1)
                    act.wait_ge(c["carry"], START + i + 1)
                    for k in range(KC):
                        ins = act.activation(y1T[:, k, 1:], T_bank[:, k, :], ACT.Identity)
                    ins.then_inc(c["y1T"], 1)

                front(0)
                turn_out(0)
                front(1)
                with act.Fori(0, B) as b:
                    for u in range(2):
                        i = b * 2 + u
                        act.wait_ge(c["k"], START + i + 1)
                        act.wait_ge(c["ka"], START + i)
                        for k in range(KC):
                            ins = act.activation(kr[:, k, :], K_bank[:, k, :], ACT.Relu)
                        ins.then_inc(c["kr"], 1)
                        act.wait_ge(c["kr"], START + i + 1)
                        act.wait_ge(c["kv"], START + i)
                        act.activation(ka[:, :, :], kr[:, :, :], ACT.Square).then_inc(c["ka"], 1)
                        front(i + 2)
                        act.wait_ge(c["r"], START + i + 1)
                        act.wait_ge(c["ff"], START + i)
                        for h in range(2):
                            ins = act.activation(r_sb[:, 2 * h:2 * h + 2, :],
                                                 R_bank[:, h, :].rearrange("p (t d) -> p t d", d=D), ACT.Sigmoid)
                        ins.then_inc(c["r_sb"], 1)
                        turn_out(i + 1)

            @block.tensor
            def _(pe):
                def rows_times(bank, src, w, done):
                    for t in range(CT):
                        for k in range(KC):
                            ins = pe.matmul(bank[:, t // 2, (t % 2) * D:(t % 2 + 1) * D],
                                            src[:, k, t * P:(t + 1) * P], w_sb[w][:, k, :],
                                            start=(k == 0), stop=(k == KC - 1))
                    ins.then_inc(done, 1)

                def turn_attn(i, u, b):
                    pe.wait_ge(c_at[u], START + 16 * NG * b + 16 * NG)
                    pe.wait_ge(c["atT"], START + i)
                    if not isinstance(i, int):
                        pe.wait_ge(c["kr"], START + i - 1)
                    for k in range(KC):
                        for t in range(CT):
                            ins = pe.transpose(K_bank[:, k, t * P:(t + 1) * P], at[:, u, t, k * P:(k + 1) * P],
                                               ident[:, :])
                    ins.then_inc(c["aT"], 1)

                def project_out(i):
                    pe.wait_ge(c["atT"], START + i + 1)
                    pe.wait_ge(c["y"], START + i)
                    if not isinstance(i, int):
                        pe.wait_ge(c["ff"], START + i - 1)
                    rows_times(N_bank, atT, "o", c["o"])

                def turn(i, u):
                    pe.wait_ge(c["y1"], START + i + 1)
                    pe.wait_ge(c["y1T"], START + i)
                    for k in range(KC):
                        for t in range(CT):
                            ins = pe.transpose(T_bank[:, k, t * P:(t + 1) * P], y1[:, u, t, k * P:(k + 1) * P],
                                               ident[:, :])
                    ins.then_inc(c["yT"], 1)

                for k in range(KC):
                    pe.matmul(N_bank[:, 1, 0:D], col[:, 4, k:k + 1].to_broadcast([P, P]), w_sb["o"][:, k, :],
                              start=(k == 0), stop=False)
                pe.matmul(N_bank[:, 1, 0:D], ones_row[:, :], bo_row[:, :], start=False, stop=True).then_inc(s_bo, 1)
                pe.wait_ge(s_bo, START + 2)
                turn_attn(0, 0, 0)
                project_out(0)
                turn(0, 0)
                turn_attn(1, 1, 0)
                project_out(1)
                with pe.Fori(0, B) as b:
                    for u in range(2):
                        i = b * 2 + u
                        pe.wait_ge(c["xk"], START + i + 1)
                        pe.wait_ge(c["kr"], START + i)
                        pe.wait_ge(c["atT"], START + i + 2)
                        for m in range(KC):
                            for k in range(KC):
                                ins = pe.matmul(K_bank[:, m, :], w_sb["kk"][:, k, m * P:(m + 1) * P],
                                                xk[:, u, k, :], start=(k == 0), stop=(k == KC - 1))
                        ins.then_inc(c["k"], 1)
                        pe.wait_ge(c["xr"], START + i + 1)
                        pe.wait_ge(c["r_sb"], START + i)
                        rows_times(R_bank, xr[:, u], "r", c["r"])
                        turn_attn(i + 2, u, b + 1)
                        pe.wait_ge(c["y"], START + i + 2)
                        pe.wait_ge(c["ka"], START + i + 1)
                        rows_times(N_bank, ka, "vv", c["kv"])
                        turn(i + 1, 1 - u)
                        project_out(i + 2)
        scope.pop().close()


def rotary_tables():
    import numpy as np
    inv = (np.float32(1.0) / np.power(np.float32(10000.0), np.arange(0, DH, 2, dtype=np.float32) / np.float32(DH)))
    angle = (np.arange(L, dtype=np.float32)[:, None] * inv.astype(np.float32)[None, :]).astype(np.float32)
    angle = angle.astype(np.float64).T
    return [np.tile(f(angle), (H, 1)).astype(np.float32) for f in (np.cos, np.sin)]


def kernel(**inputs):
    import numpy as np
    import concourse.bacc as bacc
    from concourse.bass_utils import run_bass_kernel_spmd

    def pairs_apart(a):
        a = np.asarray(a)
        return np.ascontiguousarray(np.moveaxis(a.reshape(*a.shape[:-1], H, PAIR, 2), -1, -3).reshape(a.shape))

    a = {n.removeprefix("L0_"): np.asarray(v) for n, v in inputs.items()}
    cos, sin = rotary_tables()
    ins = {
        "x": a["attn_x"], "gamma": a["attn_ln_gamma"], "beta": a["attn_ln_beta"],
        "wq": pairs_apart(a["attn_Wq"]), "bq": pairs_apart(a["attn_bq"]),
        "wk": pairs_apart(a["attn_Wk"]), "bk": pairs_apart(a["attn_bk"]),
        "wv": a["attn_Wv"], "bv": a["attn_bv"], "wo": a["attn_Wo"], "bo": a["attn_bo"],
        "wr": a["ffn_W_r"].T, "wkk": a["ffn_W_k"].T, "wvv": a["ffn_W_v"].T,
        "mu_r": a["ffn_mu_r"], "mu_k": a["ffn_mu_k"], "cos": cos, "sin": sin,
    }
    nc = bacc.Bacc("TRN2", target_bir_lowering=False, num_devices=1)
    arrays, aps = {}, {}
    for name, v in ins.items():
        v = np.ascontiguousarray(v)
        arrays[f"in_{name}"] = v
        aps[name] = nc.dram_tensor(f"in_{name}", v.shape, mybir.dt.from_np(v.dtype), kind="ExternalInput").ap()
    aps["out"] = nc.dram_tensor("out_0", (B, L, D), F32, kind="ExternalOutput").ap()
    program(nc, **aps)
    r = run_bass_kernel_spmd(nc, [arrays], core_ids=[0])
    return r.results[0]["out_0"]
```

```python
from contextlib import ExitStack

import concourse.bass as bass
from concourse import mybir

F32 = mybir.dt.float32
BF16 = mybir.dt.bfloat16
ALU = mybir.AluOpType
ACT = mybir.ActivationFunctionType
AX = mybir.AxisListType

P = 128
B, L, D = 8, 1024, 256
H, DH = 16, 16
HG = 4
NG = H // HG
NT = L // P
CH = 512
CT = CH // P
HALVES = L // CH
KC = D // P
PAIR = DH // 2
EPS = 1e-5
LOWEST = -3.0e38
START = 1
STACK = 6 * DH
SHIFT = 3
VW = 32

Q_RUNS = [(0, 0, 3), (3 * DH, 0, 2), (5 * DH, 0, 1)]
K_RUNS = [(0, 0, 1), (DH, 0, 1), (2 * DH, 0, 1), (3 * DH, 1, 1), (4 * DH, 1, 1), (5 * DH, 2, 1)]
LOADS = 16 * (len(Q_RUNS) + len(K_RUNS))

ROUNDS = [(2, 0, 384, True), (1, 0, 256, True), (0, 0, 128, True), (3, 0, 512, True),
          (4, 0, 512, False), (5, 0, 512, False), (6, 0, 512, False), (6, 1, 384, True),
          (5, 1, 256, True), (4, 1, 128, True), (7, 0, 512, False), (7, 1, 512, True)]
ITEMS = [(r, heads) for r, rd in enumerate(ROUNDS)
         for heads in ([(h,) for h in range(HG)] if 2 * rd[2] > CH else [(0, 1), (2, 3)])]
TURN_ITEM = sum(r <= 2 for r, heads in ITEMS)
UNITS = [(c, j, max(0, (j - CT * c) * P))
         for c, j in ((0, 0), (1, 0), (0, 3), (1, 1), (0, 2), (1, 2), (0, 1), (1, 3), (1, 4), (1, 7), (1, 5), (1, 6))]
NU = len(UNITS)
LAST_UNIT = [max(u for u, (c, j, o) in enumerate(UNITS) if c == k) for k in range(HALVES)]
PV_LAG = 2
SUMS_TURN = LAST_UNIT[0] + PV_LAG + 2
PRING = 4
SLOT_USES = [len(ITEMS) // 2 + 1, len(ITEMS) // 2]


PIECES = []
for _u in range(PV_LAG, NU + PV_LAG):
    _pieces = [(kind, _u - (PV_LAG if kind == "v" else 0), k) for kind in "sv" for k in range(2)]
    PIECES.append(_pieces if _u < NU + PV_LAG - 1 else _pieces[2:] + _pieces[:2])


OVERHEAD = 160
LATENCY = 150
START_BUSY = 2000


def pass1_share():
    share, pe, reduced, busy = [], 0, [0, 0], START_BUSY
    for pieces in PIECES:
        for kind, u, k in pieces:
            pe += 2 * (CH - UNITS[u % NU][2])
            share.append(0)
            while len(reduced) < 2 + len(ITEMS) and reduced[-2] <= pe:
                r, heads = ITEMS[len(reduced) - 2]
                w = ROUNDS[r][2] * len(heads)
                pe += w
                busy = max(busy, pe + LATENCY) + 2.5 * w + OVERHEAD * len(heads)
                reduced.append(busy)
                share[-1] += 1
    return share


PASS1_SHARE = pass1_share()


def program(nc, x, gamma, beta, wq, bq, wk, bk, wv, bv, wo, bo, wr, wkk, wvv, mu_r, mu_k, cos, sin, out):
    ctx = ExitStack()
    with ctx:
        scope = [ctx]

        def sb(name, shape, dt=F32):
            return scope[-1].enter_context(nc.sbuf_tensor(name, shape, dt))

        def plain_sem(name):
            return ctx.enter_context(nc.semaphore(name))

        counted = []

        def sem(name):
            counted.append(plain_sem(name))
            return counted[-1]

        def start_counters(sp):
            for s in counted:
                sp.sem_inc(s, START)
            counted.clear()

        def dram(name, shape, dt):
            return nc.dram_tensor(name, shape, dt, kind="Internal").ap()

        banks = [ctx.enter_context(nc.psum_tensor(f"bank{i}", [P, 2, CH], F32)) for i in range(4)]

        q_dram = dram("q_parts", [B, H, 3, 2, PAIR, L], BF16)
        k_dram = dram("k_parts", [B, H, 3, 2, PAIR, L], BF16)
        v_dram = dram("v_rows", [B, NG, P, NT, HG * DH], F32)
        attn_dram = dram("attn_rows", [B, NG, P, NT, HG * DH], F32)

        m_dram = dram("max_rows", [NG, SHIFT * HG * NT, P], BF16)

        x_rows = x.rearrange("b (c t p) d -> (b c) p t d", p=P, t=CT)
        out_rows = out.rearrange("b (c t p) d -> (b c) p t d", p=P, t=CT)

        ident = sb("ident", [P, P])
        ident16 = sb("ident16", [P, P], BF16)
        causal = sb("causal", [P, CH], BF16)
        cos_sb = sb("cos_sb", [P, L])
        sin_sb = sb("sin_sb", [P, L])
        w_sb = {n: sb(f"w_{n}", [P, KC, D]) for n in ("q", "k", "v", "o", "r", "kk", "vv")}
        col = sb("col", [P, 8, KC])
        bo_row = sb("bo_row", [1, D])
        ones_row = sb("ones_row", [1, P])
        bias_out = sb("bias_out", [P, D])
        epsc = sb("epsc", [P, CT])

        s_w = plain_sem("weights_loaded")
        s_wlate = plain_sem("late_weights_loaded")
        s_wc = plain_sem("vectors_loaded")
        s_c = sem("constants_set")
        s_cq = sem("scaled_bias_set")
        s_bo = sem("output_bias_sum")


        scope.append(ExitStack())
        xa = sb("xa", [P, 2, CT, D])
        xn = sb("xn", [P, 2, CT, D])
        stats = sb("stats", [P, CT, 6])
        mv = sb("mv", [P, CT, 2])
        rstd = sb("rstd", [P, CT])
        vare = sb("vare", [P, CT])
        xnT = sb("xnT", [P, 2, KC, CH])
        proj = {n: sb(f"proj_{n}", [P, 2, CH]) for n in "qk"}
        mulc = {n: sb(f"mulc_{n}", [P, 2, CH]) for n in "qk"}
        muls = {n: sb(f"muls_{n}", [P, 2, CH]) for n in "qk"}
        rot = {n: sb(f"rot_{n}", [P, 2, CH]) for n in "qk"}
        rest = {n: sb(f"rest_{n}", [P, 2, CH]) for n in "qk"}
        parts = {n: sb(f"parts_{n}", [P, 2, 3, 2, CH], BF16) for n in "qk"}
        v_sb = sb("v_sb", [P, 2, NG, CT, HG * DH])

        a_x = [sem(f"a_x_loaded{u}") for u in range(2)]
        a_stat = sem("a_stats")
        a_mv = sem("a_mean_var")
        a_eps = sem("a_var_eps")
        a_rstd = sem("a_rstd")
        a_xn = sem("a_xn")
        a_T = sem("a_turned")
        a_xnT = sem("a_xnT")
        a_p = {n: sem(f"a_{n}_projected") for n in "qkv"}
        a_e = {n: sem(f"a_{n}_evacuated") for n in "qkv"}
        a_mul = {n: sem(f"a_{n}_products") for n in "qk"}
        a_rot = {n: sem(f"a_{n}_rotated") for n in "qk"}
        a_h = {n: sem(f"a_{n}_high") for n in "qk"}
        a_r1 = {n: sem(f"a_{n}_rest") for n in "qk"}
        a_m = {n: sem(f"a_{n}_middle") for n in "qk"}
        a_l = {n: sem(f"a_{n}_low") for n in "qk"}
        a_w = {n: [sem(f"a_{n}_written{u}") for u in range(2)] for n in "qkv"}
        NP16 = 16 * 6

        turn_bank, q_bank, k_bank, v_bank = banks
        chunks = B * HALVES

        with nc.Block() as block:
            def products(eng, n, i, u):
                eng.wait_ge(a_e[n], START + i + 1)
                eng.wait_ge(a_rot[n], START + i)
                for table, dst in ((cos_sb, mulc[n]), (sin_sb, muls[n])):
                    t = table[:, u * CH:(u + 1) * CH].unsqueeze(1).to_broadcast([P, 2, CH])
                    eng.tensor_tensor(dst[:, :, :], proj[n][:, :, :], t, ALU.mult).then_inc(a_mul[n], 1)

            @block.sync
            def _(sp):
                def load_weight(n, w, done):
                    sp.dma_start(w_sb[n][:, :, :], w.rearrange("(k p) n -> p k n", p=P)).then_inc(done, 16)

                start_counters(sp)
                sp.dma_start(xa[:, 0], x_rows[0]).then_inc(a_x[0], 16)
                load_weight("k", wk, s_w)
                load_weight("q", wq, s_w)
                sp.dma_start(xa[:, 1], x_rows[1]).then_inc(a_x[1], 16)
                sp.dma_start(cos_sb[:, :], cos).then_inc(s_w, 16)
                sp.dma_start(sin_sb[:, :], sin).then_inc(s_w, 16)
                load_weight("v", wv, s_w)
                for n, w in (("o", wo), ("r", wr), ("kk", wkk), ("vv", wvv)):
                    load_weight(n, w, s_wlate)
                sp.dma_start(bo_row[:, :], bo.rearrange("(o d) -> o d", o=1)).then_inc(s_wlate, 16)
                for u in range(2):
                    sp.wait_ge(a_xn, START + u + 1)
                    sp.dma_start(xa[:, u], x_rows[u + 2]).then_inc(a_x[u], 16)
                with sp.Fori(0, B) as b:
                    for u in range(2):
                        i = b * 2 + u
                        sp.wait_ge(a_xn, START + i + 3)
                        sp.nop(nofuse=True)
                        sp.dma_start(xa[:, u], x_rows[(i + 4) & (chunks - 1)]).then_inc(a_x[u], 16)
                        toks = slice(u * CH, (u + 1) * CH)
                        sp.wait_ge(a_e["v"], START + i + 1)
                        sp.nop(nofuse=True)
                        sp.dma_start(v_dram[b, :, :, u * CT:(u + 1) * CT, :].rearrange("g p t d -> p g (t d)"),
                                     v_sb[:, u].rearrange("p g t d -> p g (t d)")).then_inc(a_w["v"][u], 16)
                        for n, dst in (("k", k_dram), ("q", q_dram)):
                            sp.wait_ge(a_l[n], START + i + 1)
                            sp.nop(nofuse=True)
                            for part in range(3):
                                for c in range(2):
                                    sp.dma_start(dst[b, :, part, c, :, toks],
                                                 parts[n][:, u, part, c, :]).then_inc(a_w[n][u], 16)
                for u in range(2):
                    sp.wait_ge(a_x[u], START + 16 * (B + 2))
                    sp.nop(nofuse=True)
                    sp.wait_ge(a_w["v"][u], START + 16 * B)
                    sp.nop(nofuse=True)
                    sp.wait_ge(a_w["q"][u], START + NP16 * B)
                    sp.nop(nofuse=True)
                    sp.wait_ge(a_w["k"][u], START + NP16 * B)
                    sp.nop(nofuse=True)

            @block.gpsimd
            def _(pool):
                for n, v in enumerate((gamma, beta, bq, bk, bv, mu_r, mu_k)):
                    with nc.allow_non_contiguous_dma(reason="256 values in all"):
                        pool.dma_start(col[:, n, :], v.rearrange("(k p) -> p k", p=P)).then_inc(s_wc, 16)
                c = [0]

                def link(ins):
                    c[0] += 1
                    ins.then_inc(s_c, 1)
                    pool.wait_ge(s_c, START + c[0])

                link(pool.memset(ident[:, :], 0.0))
                link(pool.affine_select(out=ident[:, :], in_=ident[:, :], compare_op=ALU.not_equal, fill=1.0,
                                        base=0, pattern=[[-1, P]], channel_multiplier=1))
                link(pool.tensor_copy(ident16[:, :], ident[:, :]))
                link(pool.memset(causal[:, :], 0.0))
                link(pool.affine_select(out=causal[:, CH - P:], in_=causal[:, CH - P:], compare_op=ALU.is_ge,
                                        fill=LOWEST, base=0, pattern=[[-1, P]], channel_multiplier=1))
                link(pool.memset(epsc[:, :], -0.5))
                link(pool.memset(ones_row[:, :], 1.0))
                def chunk_rstd(i):
                    pool.wait_ge(a_mv, START + i + 1)
                    pool.nop(nofuse=True)
                    pool.tensor_scalar(vare[:, :], mv[:, :, 1], EPS, 1.0, ALU.add, ALU.mult).then_inc(a_eps, 1)
                    pool.wait_ge(a_eps, START + i + 1)
                    pool.tensor_tensor(rstd[:, :], vare[:, :], epsc[:, :], ALU.pow).then_inc(a_rstd, 1)

                chunk_rstd(0)
                pool.wait_ge(s_wc, 16 * 7)
                pool.tensor_scalar(col[:, 7, :], col[:, 2, :], 0.25, 0.0, ALU.mult, ALU.add).then_inc(s_cq, 1)
                chunk_rstd(1)
                chunk_rstd(2)
                pool.wait_ge(s_w, 16 * 5)
                products(pool, "k", 0, 0)
                with pool.Fori(0, B) as b:
                    for u in range(2):
                        i = b * 2 + u
                        pool.wait_ge(a_h["k"], START + i + 1)
                        pool.wait_ge(a_m["k"], START + i)
                        pool.wait_ge(a_l["k"], START + i)
                        pool.tensor_tensor(rest["k"][:, :, :], rot["k"][:, :, :], parts["k"][:, u, 0], ALU.subtract)\
                            .then_inc(a_r1["k"], 1)
                        products(pool, "k", i + 1, 1 - u)
                        chunk_rstd(i + 3)

            @block.vector
            def _(dve):
                def chunk_stats(i, u, loads):
                    dve.wait_ge(a_x[u], START + loads)
                    for t in range(CT):
                        ins = dve.bn_stats(stats[:, t, :], xa[:, u, t, :])
                    ins.then_inc(a_stat, 1)
                    dve.wait_ge(a_stat, START + i + 1)
                    dve.nop(nofuse=True)
                    for t in range(CT):
                        ins = dve.bn_aggr(mv[:, t, :], stats[:, t, :])
                    ins.then_inc(a_mv, 1)

                def normalise(i, u):
                    dve.wait_ge(a_rstd, START + i + 1)
                    dve.wait_ge(a_mv, START + i + 1)
                    if not isinstance(i, int):
                        dve.wait_ge(a_T, START + i - 1)
                    for t in range(CT):
                        ins = dve.tensor_scalar(xn[:, u, t, :], xa[:, u, t, :], mv[:, t, 0:1], rstd[:, t:t + 1],
                                                ALU.subtract, ALU.mult)
                    ins.then_inc(a_xn, 1)

                def rotate(n, i):
                    dve.wait_ge(a_mul[n], START + 2 * i + 2)
                    dve.wait_ge(a_h[n], START + i)
                    dve.wait_ge(a_r1[n], START + i)
                    dve.tensor_tensor(rot[n][:, 0, :], mulc[n][:, 0, :], muls[n][:, 1, :], ALU.subtract)
                    dve.tensor_tensor(rot[n][:, 1, :], muls[n][:, 0, :], mulc[n][:, 1, :],
                                      ALU.add).then_inc(a_rot[n], 1)

                def rest_q(i, u):
                    dve.wait_ge(a_h["q"], START + i + 1)
                    dve.wait_ge(a_m["q"], START + i)
                    dve.tensor_tensor(rest["q"][:, :, :], rot["q"][:, :, :], parts["q"][:, u, 0], ALU.subtract)\
                       .then_inc(a_r1["q"], 1)

                def low_part(n, i, u):
                    dve.wait_ge(a_m[n], START + i + 1)
                    dve.wait_ge(a_r1[n], START + i + 1)
                    dve.tensor_tensor(parts[n][:, u, 2], rest[n][:, :, :], parts[n][:, u, 1], ALU.subtract)\
                       .then_inc(a_l[n], 1)

                chunk_stats(0, 0, 16)
                normalise(0, 0)
                chunk_stats(1, 1, 16)
                normalise(1, 1)
                chunk_stats(2, 0, 32)
                with dve.Fori(0, B) as b:
                    for u in range(2):
                        i = b * 2 + u
                        products(dve, "q", i, u)
                        rotate("k", i)
                        rotate("q", i)
                        normalise(i + 2, u)
                        rest_q(i, u)
                        chunk_stats(i + 3, 1 - u, 16 * b + 32 + 16 * u)
                        low_part("k", i, u)
                        low_part("q", i, u)

            @block.scalar
            def _(act):
                def turn_out(i, u, first):
                    act.wait_ge(a_T, START + i + 1)
                    if not first:
                        act.wait_ge(a_p["v"], START + i - 1)
                    for k in range(KC):
                        ins = act.activation(xnT[:, u, k, :], turn_bank[:, k, :], ACT.Identity,
                                             bias=col[:, 1, k:k + 1], scale=col[:, 0, k:k + 1])
                    ins.then_inc(a_xnT, 1)

                def project_out(n, i):
                    act.wait_ge(a_p[n], START + i + 1)
                    act.wait_ge(a_mul[n], START + 2 * i)
                    bank, scale, bias = (q_bank, 0.25, 7) if n == "q" else (k_bank, 1.0, 3)
                    for c in range(2):
                        ins = act.activation(proj[n][:, c, :], bank[:, c, :], ACT.Identity,
                                             bias=col[:, bias, c:c + 1], scale=scale)
                    ins.then_inc(a_e[n], 1)

                def high(n, i, b, u):
                    act.wait_ge(a_rot[n], START + i + 1)
                    act.wait_ge(a_w[n][u], START + NP16 * b)
                    act.activation(parts[n][:, u, 0], rot[n][:, :, :], ACT.Identity).then_inc(a_h[n], 1)

                def middle(n, i, u):
                    act.wait_ge(a_r1[n], START + i + 1)
                    act.activation(parts[n][:, u, 1], rest[n][:, :, :], ACT.Identity).then_inc(a_m[n], 1)

                act.wait_ge(s_wc, 16 * 7)
                act.wait_ge(s_cq, START + 1)
                turn_out(0, 0, True)
                project_out("k", 0)
                with act.Fori(0, B) as b:
                    for u in range(2):
                        i = b * 2 + u
                        project_out("q", i)
                        turn_out(i + 1, 1 - u, False)
                        high("k", i, b, u)
                        high("q", i, b, u)
                        act.wait_ge(a_p["v"], START + i + 1)
                        act.wait_ge(a_w["v"][u], START + 16 * b)
                        for t2 in range(2):
                            ins = act.activation(
                                v_sb[:, u, :, 2 * t2:2 * t2 + 2, :],
                                v_bank[:, t2, :].rearrange("p (t g d) -> p g t d", t=2, g=NG), ACT.Identity)
                        ins.then_inc(a_e["v"], 1)
                        middle("k", i, u)
                        project_out("k", i + 1)
                        middle("q", i, u)

            @block.tensor
            def _(pe):
                def turn(i, u):
                    pe.wait_ge(a_xn, START + i + 1)
                    pe.wait_ge(a_xnT, START + i)
                    for k in range(KC):
                        for t in range(CT):
                            ins = pe.transpose(turn_bank[:, k, t * P:(t + 1) * P],
                                               xn[:, u, t, k * P:(k + 1) * P], ident[:, :])
                    ins.then_inc(a_T, 1)

                def project(n, i, u):
                    pe.wait_ge(a_xnT, START + i + 1)
                    pe.wait_ge(a_e[n], START + i)
                    bank = q_bank if n == "q" else k_bank
                    for c in range(2):
                        for k in range(KC):
                            ins = pe.matmul(bank[:, c, :], w_sb[n][:, k, c * P:(c + 1) * P], xnT[:, u, k, :],
                                            start=(k == 0), stop=(k == KC - 1))
                    ins.then_inc(a_p[n], 1)

                def project_v(i, u):
                    pe.wait_ge(a_e["v"], START + i)
                    for t in range(CT):
                        for k in range(KC):
                            ins = pe.matmul(v_bank[:, t // 2, (t % 2) * D:(t % 2 + 1) * D],
                                            xnT[:, u, k, t * P:(t + 1) * P], w_sb["v"][:, k, :],
                                            start=(k == 0), stop=(k == KC - 1))
                    ins.then_inc(a_p["v"], 1)

                pe.wait_ge(s_c, START + 7)
                turn(0, 0)
                pe.wait_ge(s_w, 16 * 5)
                project("k", 0, 0)
                with pe.Fori(0, B) as b:
                    for u in range(2):
                        i = b * 2 + u
                        project("q", i, u)
                        turn(i + 1, 1 - u)
                        project_v(i, u)
                        project("k", i + 1, 1 - u)

        scope.pop().close()

        scope.append(ExitStack())
        q_st = [sb(f"q_stack{g}", [P, HG, L], BF16) for g in range(NG)]
        k_st = [sb(f"k_stack{g}", [P, HG, L], BF16) for g in range(NG)]
        v_ld = [sb(f"v_loaded{g}", [P, NT, HG * DH]) for g in range(NG)]
        v_pad = [sb(f"v_padded{g}", [P, NT, HG, VW]) for g in range(NG)]
        probs = sb("probs", [P, PRING, HG, CH])
        junk = sb("junk", [P, 2, CH], BF16)
        mx = sb("mx", [P, 2, 2, HG, NT])
        mrow = sb("mrow", [P, HG * NT])
        mrest = sb("mrest", [P, HG * NT])
        mparts = sb("mparts", [P, SHIFT, HG * NT], BF16)
        mturn = sb("mturn", [SHIFT * HG * NT, P], BF16)
        osum = sb("osum", [P, HALVES, CH])
        orec = sb("orec", [P, HALVES, CT * HG])
        oattn = sb("oattn", [P, HALVES, CT, HG * DH])

        b_init = sem("b_buffers_set")
        b_ld = [sem(f"b_stack_loaded{g}") for g in range(NG)]
        b_vld = [sem(f"b_v_loaded{g}") for g in range(NG)]
        b_v = sem("b_v_padded")
        b_s1 = [sem(f"b_scores1_done{s}") for s in range(2)]
        b_f1 = [sem(f"b_scores1_used{s}") for s in range(2)]
        b_rnd = sem("b_rounds_reduced")
        b_mc = sem("b_max_steps")
        b_mrow = [sem(f"b_max_rows_loaded{g}") for g in range(NG)]
        b_mw = sem("b_max_written")
        b_st = [sem(f"b_scores2_done{s}") for s in range(2)]
        b_ex = [sem(f"b_exp_done{s}") for s in range(2)]
        b_sel = sem("b_diagonal_cut")
        b_pv = [sem(f"b_pv_done{s}") for s in range(PRING)]
        b_os = [sem(f"b_sums_out{c}") for c in range(HALVES)]
        b_ot = [sem(f"b_sums_turned{c}") for c in range(HALVES)]
        b_rc = [sem(f"b_reciprocal{c}") for c in range(HALVES)]
        b_nm = [sem(f"b_normalised{c}") for c in range(HALVES)]
        b_aw = [sem(f"b_attn_written{c}") for c in range(HALVES)]
        MSTEPS = 5
        UPR = NU // PRING

        s1_bank = banks[0]
        s2_bank = [banks[1], banks[2]]
        acc = banks[3]
        pass1_diag = [r for r, rd in enumerate(ROUNDS) if rd[3]]
        diag_units = [u for u, (c, j, o) in enumerate(UNITS) if j // CT == c]

        with nc.Block() as block:
            @block.sync
            def _(sp):
                def load(g, b):
                    for st, src, runs in ((q_st[g], q_dram, Q_RUNS), (k_st[g], k_dram, K_RUNS)):
                        heads = src[b, g * HG:(g + 1) * HG].rearrange("h a c r n -> (a c r) h n")
                        for row, part, n in runs:
                            sp.dma_start(st[row:row + n * DH, :, :],
                                         heads[part * DH:(part + n) * DH]).then_inc(b_ld[g], 16)
                    sp.dma_start(v_ld[g][:, :, :], v_dram[b, g]).then_inc(b_vld[g], 16)

                def load_max_rows(g, p):
                    sp.wait_ge(b_f1[0], START + SLOT_USES[0] * p + TURN_ITEM // 2 + 1)
                    sp.nop(nofuse=True)
                    sp.dma_start(m_dram[g], mturn[:, :]).then_inc(b_mw, 16)
                    sp.wait_ge(b_mw, START + 16 * p)
                    sp.nop(nofuse=True)
                    sp.dma_start(q_st[g][STACK:STACK + SHIFT].rearrange("s h t -> s (h t)"),
                                 m_dram[g].rearrange("(s r) n -> s (r n)", s=SHIFT)).then_inc(b_mrow[g], 16)

                start_counters(sp)
                for g in range(3):
                    load(g, 0)
                load_max_rows(0, 1)
                with sp.Fori(0, B) as b:
                    nb = (b + 1) & (B - 1)
                    for g in range(NG):
                        n = b * NG + g
                        sp.wait_ge(b_st[1], START + NU * n)
                        sp.nop(nofuse=True)
                        sp.wait_ge(b_pv[PRING - 1], START + UPR * n)
                        sp.nop(nofuse=True)
                        load((g + 3) % NG, b if g == 0 else nb)
                        load_max_rows((g + 1) % NG, n + 2)
                        for c in range(HALVES):
                            sp.wait_ge(b_nm[c], START + n + 1)
                            sp.nop(nofuse=True)
                            sp.dma_start(attn_dram[b, g, :, c * CT:(c + 1) * CT, :], oattn[:, c])\
                              .then_inc(b_aw[c], 16)
                for c in range(HALVES):
                    sp.wait_ge(b_aw[c], START + 16 * B * NG)
                    sp.nop(nofuse=True)
                for g in range(NG):
                    loads = B + 1 if g < 3 else B
                    sp.wait_ge(b_ld[g], START + LOADS * loads)
                    sp.nop(nofuse=True)
                    sp.wait_ge(b_vld[g], START + 16 * loads)
                    sp.nop(nofuse=True)
                sp.wait_ge(b_mrow[0], START + 16 * (B + 1))

            @block.gpsimd
            def _(pool):
                for g in range(NG):
                    pool.memset(v_pad[g][:, :, :, DH:], 1.0)
                pool.memset(mparts[:, :, :], 0.0).then_inc(b_init, 1)
                pool.wait_ge(b_init, START + 1)
                for g in range(NG):
                    pool.memset(k_st[g][STACK:STACK + SHIFT], 1.0).then_inc(b_init, 1)
                pool.wait_ge(b_init, START + 1 + NG)

                def pad_v(g, loads):
                    pool.wait_ge(b_vld[g], START + 16 * loads)
                    pool.nop(nofuse=True)
                    pool.tensor_scalar(v_pad[g][:, :, :, 0:DH],
                                       v_ld[g][:, :, :].rearrange("p t (h d) -> p t h d", h=HG),
                                       1.0, 1.0, ALU.mult, ALU.mult).then_inc(b_v, 1)

                def cut_diagonal(n, u):
                    for s in range(2):
                        pool.wait_ge(b_ex[s], START + NU * n + u + 1)
                        pool.nop(nofuse=True)
                    tile = probs[:, u % PRING, :, 0:P]
                    pool.affine_select(out=tile, in_=tile, compare_op=ALU.is_ge, fill=0.0, base=0,
                                       pattern=[[0, HG], [1, P]], channel_multiplier=-1).then_inc(b_sel, 1)

                for g in range(3):
                    pad_v(g, 1)
                for u in range(PV_LAG):
                    if u in diag_units:
                        cut_diagonal(0, u)
                with pool.Fori(0, B) as b:
                    for g in range(NG):
                        n = b * NG + g
                        for u in range(PV_LAG, NU + PV_LAG):
                            if u % NU in diag_units:
                                cut_diagonal(n + u // NU, u % NU)
                        pad_v((g + 3) % NG, b + 1 if g == 0 else b + 2)

            @block.vector
            def _(dve):
                def take_maxima(m, parity, normal, chain):
                    def split_step(k):
                        last = mx[:, 1 - parity]
                        if k == 0:
                            dve.wait_ge(b_f1[0], START + m * SLOT_USES[0])
                            dve.wait_ge(b_f1[1], START + m * SLOT_USES[1])
                            ins = dve.tensor_tensor(mrow[:, :], last[:, 0].rearrange("p h t -> p (h t)"),
                                                    last[:, 1].rearrange("p h t -> p (h t)"), ALU.max)
                        else:
                            dve.wait_ge(b_mc, START + (m - 1) * MSTEPS + k)
                        if k == 1:
                            ins = dve.tensor_scalar(mparts[:, 0], mrow[:, :], -1.0, None, ALU.mult)
                        if k == 2:
                            ins = dve.scalar_tensor_tensor(out=mrest[:, :], in0=mrow[:, :], scalar=-1.0,
                                                           in1=mparts[:, 0], op0=ALU.mult, op1=ALU.subtract)
                        if k == 3:
                            ins = dve.tensor_copy(mparts[:, 1], mrest[:, :])
                        if k == 4:
                            ins = dve.tensor_tensor(mparts[:, 2], mrest[:, :], mparts[:, 1], ALU.subtract)
                        ins.then_inc(b_mc, 1)

                    for k, (r, heads) in enumerate(ITEMS):
                        t, half, w, masked = ROUNDS[r]
                        s = k % 2
                        done = k // 2 + 1 + (1 if s == 0 and k >= TURN_ITEM else 0)
                        dve.wait_ge(b_s1[s], START + m * SLOT_USES[s] + done)
                        dve.nop(nofuse=True)
                        for e, h in enumerate(heads):
                            dst = mx[:, parity, half, h, t:t + 1]
                            scores = s1_bank[:, s, e * w:(e + 1) * w]
                            if masked:
                                ins = dve.tensor_tensor_reduce(junk[:, s, e * w:(e + 1) * w], scores,
                                                               causal[:, CH - w:], 1.0, LOWEST, ALU.add, ALU.max, dst)
                            else:
                                ins = dve.tensor_reduce(dst, scores, AX.X, ALU.max)
                        ins.then_inc(b_f1[s], 1)
                        if chain and 1 <= k <= MSTEPS:
                            split_step(k - 1)
                        if k == TURN_ITEM - 1:
                            dve.wait_ge(b_s1[0], START + m * SLOT_USES[0] + TURN_ITEM // 2 + 1)
                            dve.tensor_copy(mturn[:, :], s1_bank[0:SHIFT * HG * NT, 0, 0:P // 2].bitcast(BF16))\
                               .then_inc(b_f1[0], 1)
                        if normal is not None and k == len(ITEMS) - HG - 1:
                            normal(0)
                    if normal is not None:
                        normal(1)

                for parity in range(2):
                    dve.memset(mx[:, parity, 1, :, 0:CT], LOWEST)
                take_maxima(0, 0, None, False)
                take_maxima(1, 1, None, True)
                with dve.Fori(0, B) as b:
                    for g in range(NG):
                        n = b * NG + g

                        def normal(c):
                            turned = acc[:, c, :].rearrange("p (s w) -> p s w", w=VW)
                            dve.wait_ge(b_ot[c], START + n + 1)
                            dve.reciprocal(orec[:, c, :], turned[:, :, DH]).then_inc(b_rc[c], 1)
                            dve.wait_ge(b_rc[c], START + n + 1)
                            dve.wait_ge(b_aw[c], START + 16 * n)
                            dve.tensor_tensor(oattn[:, c].rearrange("p t (h d) -> p (t h) d", h=HG),
                                              turned[:, :, 0:DH],
                                              orec[:, c, :].unsqueeze(2).to_broadcast([P, CT * HG, DH]),
                                              ALU.mult).then_inc(b_nm[c], 1)

                        take_maxima(n + 2, g % 2, normal, True)

            @block.scalar
            def _(act):
                def sums_out(c, n):
                    last = LAST_UNIT[c]
                    act.wait_ge(b_pv[last % PRING], START + UPR * n + last // PRING + 1)
                    act.wait_ge(b_ot[c], START + n)
                    act.activation(osum[:, c, :], acc[:, c, :], ACT.Identity).then_inc(b_os[c], 1)

                def exponentials(n, u):
                    o = UNITS[u][2]
                    act.wait_ge(b_pv[u % PRING], START + UPR * n + u // PRING)
                    for s in range(2):
                        act.wait_ge(b_st[s], START + NU * n + u + 1)
                        act.activation(probs[:, u % PRING, 2 * s:2 * s + 2, 0:CH - o],
                                       s2_bank[s][:, :, 0:CH - o], ACT.Exp).then_inc(b_ex[s], 1)

                for u in range(PV_LAG):
                    exponentials(0, u)
                with act.Fori(0, B) as b:
                    for g in range(NG):
                        n = b * NG + g
                        for u in range(PV_LAG, NU + PV_LAG):
                            if u == NU + PV_LAG - 1:
                                sums_out(1, n)
                            exponentials(n + u // NU, u % NU)
                            if u == LAST_UNIT[0] + PV_LAG:
                                sums_out(0, n)

            @block.tensor
            def _(pe):
                def pass1(m, g, items):
                    for k in items:
                        r, heads = ITEMS[k]
                        t, half, w, _ = ROUNDS[r]
                        s = k % 2
                        used = k // 2 + (1 if s == 0 and k >= TURN_ITEM else 0)
                        pe.wait_ge(b_f1[s], START + m * SLOT_USES[s] + used)
                        for e, h in enumerate(heads):
                            ins = pe.matmul(s1_bank[:, s, e * w:(e + 1) * w], q_st[g][0:STACK, h, t * P:(t + 1) * P],
                                            k_st[g][0:STACK, h, half * CH:half * CH + w], start=True, stop=True)
                        ins.then_inc(b_s1[s], 1)
                        if k == TURN_ITEM - 1:
                            pe.wait_ge(b_f1[0], START + m * SLOT_USES[0] + TURN_ITEM // 2)
                            pe.wait_ge(b_mc, START + m * MSTEPS)
                            pe.transpose(s1_bank[0:SHIFT * HG * NT, 0, 0:P // 2].bitcast(BF16),
                                         mparts[:, :, :].rearrange("p s n -> p (s n)"), ident16[:, :])\
                              .then_inc(b_s1[0], 1)

                pe.wait_ge(b_init, START + 1)
                for m in range(2):
                    pe.wait_ge(b_ld[m], START + LOADS)
                    pass1(m, m, range(len(ITEMS)))

                def scores2(n, g, u, s):
                    c, j, o = UNITS[u]
                    pe.wait_ge(b_ex[s], START + NU * n + u)
                    for h in (2 * s, 2 * s + 1):
                        ins = pe.matmul(s2_bank[s][:, h % 2, 0:CH - o],
                                        k_st[g][0:STACK + SHIFT, h, j * P:(j + 1) * P],
                                        q_st[g][0:STACK + SHIFT, h, c * CH + o:(c + 1) * CH],
                                        start=True, stop=True)
                    ins.then_inc(b_st[s], 1)

                pe.wait_ge(b_init, START + 1 + NG)
                pe.wait_ge(b_mrow[0], START + 16)
                for u in range(PV_LAG):
                    for s in range(2):
                        scores2(0, 0, u, s)
                with pe.Fori(0, B) as b:
                    for g in range(NG):
                        n = b * NG + g
                        g1 = (g + 1) % NG
                        g2 = (g + 2) % NG

                        def pv(u, half):
                            c, j, o = UNITS[u]
                            w = (CH - o) // 2
                            if half == 0:
                                if j == 0:
                                    pe.wait_ge(b_nm[c], START + n)
                                for s in range(2):
                                    pe.wait_ge(b_ex[s], START + NU * n + u + 1)
                                if u in diag_units:
                                    pe.wait_ge(b_sel, START + len(diag_units) * n + diag_units.index(u) + 1)
                            for h in range(HG):
                                ins = pe.matmul(acc[32 * h:32 * h + VW, c, o + half * w:o + (half + 1) * w],
                                                v_pad[g][:, j, h, :],
                                                probs[:, u % PRING, h, half * w:(half + 1) * w],
                                                start=(j == 0 and half == 0), stop=(u == LAST_UNIT[c]),
                                                skip_group_check=True)
                            if half == 1:
                                ins.then_inc(b_pv[u % PRING], 1)

                        def turn_sums(c):
                            pe.wait_ge(b_os[c], START + n + 1)
                            for t in range(CT):
                                ins = pe.transpose(acc[:, c, t * P:(t + 1) * P], osum[:, c, t * P:(t + 1) * P],
                                                   ident[:, :])
                            ins.then_inc(b_ot[c], 1)

                        pe.wait_ge(b_ld[g2], START + (LOADS * (b + 1) if g < 2 else LOADS * (b + 2)))
                        pe.wait_ge(b_v, START + n + 1)
                        m = n + 2
                        placed, piece = 0, 0
                        for pieces in PIECES:
                            for kind, u, k in pieces:
                                if kind == "v":
                                    pv(u, k)
                                elif u < NU:
                                    scores2(n, g, u, k)
                                else:
                                    if u == NU and k == 0:
                                        pe.wait_ge(b_mrow[g1], START + (16 * (b + 1) if g < 3 else 16 * (b + 2)))
                                    scores2(n + 1, g1, u - NU, k)
                                upto = placed + PASS1_SHARE[piece]
                                pass1(m, g2, range(placed, upto))
                                placed = upto
                                piece += 1
                            if ("v", SUMS_TURN - PV_LAG, 1) in pieces:
                                turn_sums(0)
                        pass1(m, g2, range(placed, len(ITEMS)))
                        turn_sums(1)

        scope.pop().close()

        scope.append(ExitStack())
        x_c = sb("x_c", [P, 2, CT, D])
        at = sb("at", [P, 2, CT, D])
        atT = sb("atT", [P, KC, CH])
        x2b = sb("x2b", [P, CT, D])
        x2 = sb("x2", [P, CT, D])
        y = sb("y", [P, CT, D])
        y1 = sb("y1", [P, 2, CT, D])
        y1T = sb("y1T", [P, KC, CH + 1])
        dx = sb("dx", [P, KC, CH])
        xr = sb("xr", [P, 2, KC, CH])
        xk = sb("xk", [P, 2, KC, CH])
        r_sb = sb("r_sb", [P, CT, D])
        kr = sb("kr", [P, KC, CH])
        ka = sb("ka", [P, KC, CH])
        ff = sb("ff", [P, CT, D])
        z = sb("z", [P, CT, D])
        zo = sb("zo", [P, 2, CT, D])
        st1 = sb("st1", [P, CT, 6])
        mv1 = sb("mv1", [P, CT, 2])
        ve1 = sb("ve1", [P, CT])
        rs1 = sb("rs1", [P, CT])
        st2 = sb("st2", [P, CT, 6])
        mv2 = sb("mv2", [P, CT, 2])
        ve2 = sb("ve2", [P, CT])
        rs2 = sb("rs2", [P, CT])

        names = ["x2", "x2b", "aT", "atT", "o", "y", "st1", "mv1", "ve1", "rs1", "y1", "yT", "y1T", "carry", "dx",
                 "xk", "xr", "r", "r_sb", "k", "kr", "ka", "kv", "ff", "z", "st2", "mv2", "ve2", "rs2"]
        c_x = [sem(f"c_x_loaded{u}") for u in range(2)]
        c_at = [sem(f"c_attn_loaded{u}") for u in range(2)]
        c_out = [sem(f"c_written{u}") for u in range(2)]
        c_zo = sem("c_zo")
        c = {n: sem(f"c_{n}") for n in names}
        T_bank, N_bank, R_bank, K_bank = banks

        with nc.Block() as block:
            @block.sync
            def _(sp):
                def load_x(i, u):
                    sp.dma_start(x_c[:, u], x_rows[i]).then_inc(c_x[u], 16)

                def load_attn(b, u):
                    for g in range(NG):
                        sp.dma_start(at[:, u, :, g * HG * DH:(g + 1) * HG * DH],
                                     attn_dram[b, g, :, u * CT:(u + 1) * CT, :]).then_inc(c_at[u], 16)

                start_counters(sp)
                for u in range(2):
                    load_attn(0, u)
                    load_x(u, u)
                for u in range(2):
                    sp.wait_ge(c["aT"], START + u + 1)
                    load_attn(1, u)
                    sp.wait_ge(c["x2"], START + u + 1)
                    load_x(u + 2, u)
                with sp.Fori(0, B) as b:
                    for u in range(2):
                        i = b * 2 + u
                        sp.wait_ge(c["aT"], START + i + 3)
                        sp.nop(nofuse=True)
                        load_attn((b + 2) & (B - 1), u)
                        sp.wait_ge(c["x2"], START + i + 3)
                        sp.nop(nofuse=True)
                        load_x((i + 4) & (chunks - 1), u)
                        sp.wait_ge(c_zo, START + i + 1)
                        sp.nop(nofuse=True)
                        sp.dma_start(out_rows[i], zo[:, u]).then_inc(c_out[u], 16)
                for u in range(2):
                    sp.wait_ge(c_out[u], START + 16 * B)
                    sp.nop(nofuse=True)
                    sp.wait_ge(c_x[u], START + 16 * (B + 2))
                    sp.nop(nofuse=True)
                    sp.wait_ge(c_at[u], START + 16 * NG * (B + 2))
                    sp.nop(nofuse=True)

            def rsqrt(eng, i, tag, mvt, vet, rst):
                eng.wait_ge(c["mv" + tag], START + i + 1)
                eng.nop(nofuse=True)
                eng.tensor_scalar(vet[:, :], mvt[:, :, 1], EPS, 1.0, ALU.add, ALU.mult).then_inc(c["ve" + tag], 1)
                eng.wait_ge(c["ve" + tag], START + i + 1)
                eng.tensor_tensor(rst[:, :], vet[:, :], epsc[:, :], ALU.pow).then_inc(c["rs" + tag], 1)

            @block.gpsimd
            def _(pool):
                def residual(i, u, b):
                    pool.wait_ge(c_x[u], START + 16 * b + 16)
                    pool.nop(nofuse=True)
                    pool.wait_ge(c["y"], START + i)
                    pool.nop(nofuse=True)
                    pool.tensor_scalar(x2[:, :, :], x_c[:, u], 2.0, 1.0, ALU.mult, ALU.mult).then_inc(c["x2"], 1)
                    pool.wait_ge(c["x2"], START + i + 1)
                    pool.tensor_tensor(x2b[:, :, :], x2[:, :, :],
                                       bias_out[:, :].unsqueeze(1).to_broadcast([P, CT, D]), ALU.add)\
                        .then_inc(c["x2b"], 1)

                pool.wait_ge(s_bo, START + 2)
                residual(0, 0, 0)
                rsqrt(pool, 0, "1", mv1, ve1, rs1)
                residual(1, 1, 0)
                rsqrt(pool, 1, "1", mv1, ve1, rs1)
                with pool.Fori(0, B) as b:
                    for u in range(2):
                        i = b * 2 + u
                        residual(i + 2, u, b + 1)
                        pool.wait_ge(c["ff"], START + i + 1)
                        pool.tensor_tensor(z[:, :, :], ff[:, :, :], y1[:, u], ALU.add).then_inc(c["z"], 1)
                        rsqrt(pool, i + 2, "1", mv1, ve1, rs1)
                        rsqrt(pool, i, "2", mv2, ve2, rs2)

            @block.vector
            def _(dve):
                def stats_of(src, i, tag, stt, mvt):
                    for t in range(CT):
                        ins = dve.bn_stats(stt[:, t, :], src[:, t, :])
                    ins.then_inc(c["st" + tag], 1)
                    dve.wait_ge(c["st" + tag], START + i + 1)
                    dve.nop(nofuse=True)
                    dve.wait_ge(c["rs" + tag], START + i)
                    dve.nop(nofuse=True)
                    for t in range(CT):
                        ins = dve.bn_aggr(mvt[:, t, :], stt[:, t, :])
                    ins.then_inc(c["mv" + tag], 1)

                def front(i):
                    dve.wait_ge(c["x2b"], START + i + 1)
                    dve.wait_ge(c["y1"], START + i)
                    dve.wait_ge(c["o"], START + i + 1)
                    for h in range(2):
                        ins = dve.tensor_tensor(
                            y[:, 2 * h:2 * h + 2, :], N_bank[:, h, :].rearrange("p (t d) -> p t d", d=D),
                            x2b[:, 2 * h:2 * h + 2, :], ALU.add)
                    ins.then_inc(c["y"], 1)
                    dve.wait_ge(c["y"], START + i + 1)
                    stats_of(y, i, "1", st1, mv1)

                def normal1(i, u, batch_start):
                    dve.wait_ge(c["xr"], START + i)
                    if batch_start:
                        dve.memset(y1T[:, :, 0:1], 0.0).then_inc(c["carry"], 1)
                    else:
                        dve.tensor_copy(y1T[:, :, 0:1], y1T[:, :, CH:CH + 1]).then_inc(c["carry"], 1)
                    dve.wait_ge(c["rs1"], START + i + 1)
                    dve.wait_ge(c["mv1"], START + i + 1)
                    for t in range(CT):
                        ins = dve.tensor_scalar(y1[:, u, t, :], y[:, t, :], mv1[:, t, 0:1], rs1[:, t:t + 1],
                                                ALU.subtract, ALU.mult)
                    ins.then_inc(c["y1"], 1)

                def mix(i, u):
                    dve.wait_ge(c["y1T"], START + i + 1)
                    dve.wait_ge(c["carry"], START + i + 1)
                    dve.tensor_tensor(dx[:, :, :], y1T[:, :, 1:], y1T[:, :, 0:CH], ALU.subtract)\
                       .then_inc(c["dx"], 1)
                    dve.wait_ge(c["dx"], START + i + 1)
                    for mu, dst, done in ((6, xk, "xk"), (5, xr, "xr")):
                        for k in range(KC):
                            ins = dve.scalar_tensor_tensor(out=dst[:, u, k, :], in0=dx[:, k, :],
                                                           scalar=col[:, mu, k:k + 1], in1=y1T[:, k, 0:CH],
                                                           op0=ALU.mult, op1=ALU.add)
                        ins.then_inc(c[done], 1)

                dve.wait_ge(s_bo, START + 1)
                dve.tensor_copy(bias_out[:, :], N_bank[:, 1, 0:D]).then_inc(s_bo, 1)
                front(0)
                normal1(0, 0, True)
                mix(0, 0)
                front(1)
                normal1(1, 1, False)
                with dve.Fori(0, B) as b:
                    for u in range(2):
                        i = b * 2 + u
                        dve.wait_ge(c["kv"], START + i + 1)
                        dve.wait_ge(c["r_sb"], START + i + 1)
                        for h in range(2):
                            ins = dve.tensor_tensor(
                                ff[:, 2 * h:2 * h + 2, :], N_bank[:, h, :].rearrange("p (t d) -> p t d", d=D),
                                r_sb[:, 2 * h:2 * h + 2, :], ALU.mult)
                        ins.then_inc(c["ff"], 1)
                        mix(i + 1, 1 - u)
                        front(i + 2)
                        dve.wait_ge(c["z"], START + i + 1)
                        stats_of(z, i, "2", st2, mv2)
                        normal1(i + 2, u, u == 0)
                        dve.wait_ge(c["rs2"], START + i + 1)
                        dve.wait_ge(c["mv2"], START + i + 1)
                        dve.wait_ge(c_out[u], START + 16 * b)
                        for t in range(CT):
                            ins = dve.tensor_scalar(zo[:, u, t, :], z[:, t, :], mv2[:, t, 0:1], rs2[:, t:t + 1],
                                                    ALU.subtract, ALU.mult)
                        ins.then_inc(c_zo, 1)

            @block.scalar
            def _(act):
                def front(i):
                    act.wait_ge(c["aT"], START + i + 1)
                    act.wait_ge(c["o"], START + i)
                    for k in range(KC):
                        ins = act.activation(atT[:, k, :], K_bank[:, k, :], ACT.Identity)
                    ins.then_inc(c["atT"], 1)

                def turn_out(i):
                    act.wait_ge(c["yT"], START + i + 1)
                    act.wait_ge(c["carry"], START + i + 1)
                    for k in range(KC):
                        ins = act.activation(y1T[:, k, 1:], T_bank[:, k, :], ACT.Identity)
                    ins.then_inc(c["y1T"], 1)

                front(0)
                front(1)
                turn_out(0)
                with act.Fori(0, B) as b:
                    for u in range(2):
                        i = b * 2 + u
                        act.wait_ge(c["k"], START + i + 1)
                        act.wait_ge(c["ka"], START + i)
                        for k in range(KC):
                            ins = act.activation(kr[:, k, :], K_bank[:, k, :], ACT.Relu)
                        ins.then_inc(c["kr"], 1)
                        act.wait_ge(c["kr"], START + i + 1)
                        act.wait_ge(c["kv"], START + i)
                        act.activation(ka[:, :, :], kr[:, :, :], ACT.Square).then_inc(c["ka"], 1)
                        front(i + 2)
                        act.wait_ge(c["r"], START + i + 1)
                        act.wait_ge(c["ff"], START + i)
                        for h in range(2):
                            ins = act.activation(r_sb[:, 2 * h:2 * h + 2, :],
                                                 R_bank[:, h, :].rearrange("p (t d) -> p t d", d=D), ACT.Sigmoid)
                        ins.then_inc(c["r_sb"], 1)
                        turn_out(i + 1)

            @block.tensor
            def _(pe):
                def rows_times(bank, src, w, done):
                    for t in range(CT):
                        for k in range(KC):
                            ins = pe.matmul(bank[:, t // 2, (t % 2) * D:(t % 2 + 1) * D],
                                            src[:, k, t * P:(t + 1) * P], w_sb[w][:, k, :],
                                            start=(k == 0), stop=(k == KC - 1))
                    ins.then_inc(done, 1)

                def turn_attn(i, u, b):
                    pe.wait_ge(c_at[u], START + 16 * NG * b + 16 * NG)
                    pe.wait_ge(c["atT"], START + i)
                    if not isinstance(i, int):
                        pe.wait_ge(c["kr"], START + i - 1)
                    for k in range(KC):
                        for t in range(CT):
                            ins = pe.transpose(K_bank[:, k, t * P:(t + 1) * P], at[:, u, t, k * P:(k + 1) * P],
                                               ident[:, :])
                    ins.then_inc(c["aT"], 1)

                def project_out(i):
                    pe.wait_ge(c["atT"], START + i + 1)
                    pe.wait_ge(c["y"], START + i)
                    if not isinstance(i, int):
                        pe.wait_ge(c["ff"], START + i - 1)
                    rows_times(N_bank, atT, "o", c["o"])

                def turn(i, u):
                    pe.wait_ge(c["y1"], START + i + 1)
                    pe.wait_ge(c["y1T"], START + i)
                    for k in range(KC):
                        for t in range(CT):
                            ins = pe.transpose(T_bank[:, k, t * P:(t + 1) * P], y1[:, u, t, k * P:(k + 1) * P],
                                               ident[:, :])
                    ins.then_inc(c["yT"], 1)

                pe.wait_ge(s_wlate, 16 * 5)
                for k in range(KC):
                    pe.matmul(N_bank[:, 1, 0:D], col[:, 4, k:k + 1].to_broadcast([P, P]), w_sb["o"][:, k, :],
                              start=(k == 0), stop=False)
                pe.matmul(N_bank[:, 1, 0:D], ones_row[:, :], bo_row[:, :], start=False, stop=True).then_inc(s_bo, 1)
                pe.wait_ge(s_bo, START + 2)
                turn_attn(0, 0, 0)
                project_out(0)
                turn_attn(1, 1, 0)
                project_out(1)
                turn(0, 0)
                with pe.Fori(0, B) as b:
                    for u in range(2):
                        i = b * 2 + u
                        pe.wait_ge(c["xk"], START + i + 1)
                        pe.wait_ge(c["kr"], START + i)
                        pe.wait_ge(c["atT"], START + i + 2)
                        for m in range(KC):
                            for k in range(KC):
                                ins = pe.matmul(K_bank[:, m, :], w_sb["kk"][:, k, m * P:(m + 1) * P],
                                                xk[:, u, k, :], start=(k == 0), stop=(k == KC - 1))
                        ins.then_inc(c["k"], 1)
                        pe.wait_ge(c["xr"], START + i + 1)
                        pe.wait_ge(c["r_sb"], START + i)
                        rows_times(R_bank, xr[:, u], "r", c["r"])
                        turn_attn(i + 2, u, b + 1)
                        pe.wait_ge(c["y"], START + i + 2)
                        pe.wait_ge(c["ka"], START + i + 1)
                        rows_times(N_bank, ka, "vv", c["kv"])
                        turn(i + 1, 1 - u)
                        project_out(i + 2)
        scope.pop().close()


def rotary_tables():
    import numpy as np
    inv = (np.float32(1.0) / np.power(np.float32(10000.0), np.arange(0, DH, 2, dtype=np.float32) / np.float32(DH)))
    angle = (np.arange(L, dtype=np.float32)[:, None] * inv.astype(np.float32)[None, :]).astype(np.float32)
    angle = angle.astype(np.float64).T
    return [np.tile(f(angle), (H, 1)).astype(np.float32) for f in (np.cos, np.sin)]


def kernel(**inputs):
    import numpy as np
    import concourse.bacc as bacc
    from concourse.bass_utils import run_bass_kernel_spmd

    def pairs_apart(a):
        a = np.asarray(a)
        return np.ascontiguousarray(np.moveaxis(a.reshape(*a.shape[:-1], H, PAIR, 2), -1, -3).reshape(a.shape))

    a = {n.removeprefix("L0_"): np.asarray(v) for n, v in inputs.items()}
    cos, sin = rotary_tables()
    ins = {
        "x": a["attn_x"], "gamma": a["attn_ln_gamma"], "beta": a["attn_ln_beta"],
        "wq": pairs_apart(a["attn_Wq"]), "bq": pairs_apart(a["attn_bq"]),
        "wk": pairs_apart(a["attn_Wk"]), "bk": pairs_apart(a["attn_bk"]),
        "wv": a["attn_Wv"], "bv": a["attn_bv"], "wo": a["attn_Wo"], "bo": a["attn_bo"],
        "wr": a["ffn_W_r"].T, "wkk": a["ffn_W_k"].T, "wvv": a["ffn_W_v"].T,
        "mu_r": a["ffn_mu_r"], "mu_k": a["ffn_mu_k"], "cos": cos, "sin": sin,
    }
    nc = bacc.Bacc("TRN2", target_bir_lowering=False, num_devices=1)
    arrays, aps = {}, {}
    for name, v in ins.items():
        v = np.ascontiguousarray(v)
        arrays[f"in_{name}"] = v
        aps[name] = nc.dram_tensor(f"in_{name}", v.shape, mybir.dt.from_np(v.dtype), kind="ExternalInput").ap()
    aps["out"] = nc.dram_tensor("out_0", (B, L, D), F32, kind="ExternalOutput").ap()
    program(nc, **aps)
    r = run_bass_kernel_spmd(nc, [arrays], core_ids=[0])
    return r.results[0]["out_0"]
```
